# Optimizing a Trainium2 kernel written in Bass

```python
import numpy as np
import jax
import jax.numpy as jnp

def _softmax(x, axis=-1):
    return jax.nn.softmax(x, axis=axis)

def _gelu(x):
    return jax.nn.gelu(x, approximate=True)

def _silu(x):
    return jax.nn.silu(x)

def _sigmoid(x):
    return jax.nn.sigmoid(x)

def _layernorm(x, axis=-1, eps=1e-05):
    m = jnp.mean(x, axis=axis, keepdims=True)
    v = jnp.var(x, axis=axis, keepdims=True)
    return (x - m) / jnp.sqrt(v + eps)

def _scatter_add(tgt, idx, src, axis=0):
    return tgt.at[idx].add(src)

def _segment_sum(src, seg, n):
    return jax.ops.segment_sum(src, seg, n)
kernel_name = 'mk_flamingo_gated_d1_seqx_r4_082194'

def setup_inputs(seed: int=0):
    np.random.seed(seed)
    _w = jnp.asarray

    def _rec_inputs():
        import jax
        import jax.numpy as jnp
        _rk = jax.random.key(seed)
        x = -0.0003929 + 0.9999 * jax.random.normal(jax.random.fold_in(_rk, 1), (16, 128, 1024), jnp.float32)
        _lenS = 128 - jax.random.randint(jax.random.fold_in(_rk, 7), (16,), 0, max(1, 128 // 4) + 1, jnp.int32)
        _lenS2 = 128 - jax.random.randint(jax.random.fold_in(_rk, 8), (16,), 0, max(1, 128 // 4) + 1, jnp.int32)
        _ctx_4096P = jax.random.normal(jax.random.fold_in(_rk, 11), (16, 16, 1024), jnp.float32)
        _ctx_4096c = jax.random.dirichlet(jax.random.fold_in(_rk, 511), 0.3 * jnp.ones((16,), jnp.float32), (16, 128))
        _ctx_4096t = jnp.einsum('bsk,bkd->bsd', _ctx_4096c, _ctx_4096P)
        _ctx_4096t = _ctx_4096t * jax.lax.rsqrt(jnp.mean(jnp.square(_ctx_4096t)) + 1e-12) * 0.953939
        ctx_4096 = 2.81802e-05 + 1.00001 * (_ctx_4096t + 0.3 * jax.random.normal(jax.random.fold_in(_rk, 611), (16, 128, 1024), jnp.float32))
        _g = jax.random.normal(jax.random.fold_in(_rk, 9001), (2, 1), jnp.float32)
        _g = jnp.sign(_g) * jnp.maximum(jnp.abs(_g), 1.0) + (_g == 0) * 1.0
        g_xattn = _g[0]
        g_ffn = _g[1]
        return (x, ctx_4096, g_xattn, g_ffn)
    x, ctx_4096, g_xattn, g_ffn = _rec_inputs()

    def _L0_xattn_setup():
        import jax, jax.numpy as jnp
        import numpy as np
        EMB_DIM = 128
        HEADS = 8
        key = jax.random.key(seed)
        kq, kk, kv = jax.random.split(key, 3)
        B, C, N = (8, EMB_DIM, 1024)
        q = jax.random.normal(kq, (B, C, N), dtype=jnp.float32)
        k = jax.random.normal(kk, (B, C, N), dtype=jnp.float32)
        v = jax.random.normal(kv, (B, C, N), dtype=jnp.float32)
        return {'q': q, 'k': k, 'v': v}
    _L0_xattn_all = _L0_xattn_setup()
    _L0_xattn_in = {k: v for k, v in _L0_xattn_all.items() if k in ()}
    del _L0_xattn_all

    def _L0_ffn_setup():
        import jax, jax.numpy as jnp
        import numpy as np
        K_TOP = 8
        key = jax.random.key(seed)
        k1, k2, k3 = jax.random.split(key, 3)
        B, S, H, E = (4, 1024, 1024, 64)
        hidden_states = jax.random.normal(k1, (B, S, H), dtype=jnp.float32)
        router_weight = jax.random.normal(k2, (E, H), dtype=jnp.float32)
        router_bias = jnp.zeros((E,), dtype=jnp.float32)
        expert_bias = jax.random.normal(k3, (E, H), dtype=jnp.float32) * 0.1
        return {'hidden_states': hidden_states, 'router_weight': router_weight, 'router_bias': router_bias, 'expert_bias': expert_bias}
    _L0_ffn_all = _L0_ffn_setup()
    _L0_ffn_in = {k: v for k, v in _L0_ffn_all.items() if k in ('router_weight', 'router_bias', 'expert_bias')}
    del _L0_ffn_all
    return {'x': x, 'ctx_4096': ctx_4096, 'g_xattn': g_xattn, 'g_ffn': g_ffn, 'L0_ffn_router_weight': _L0_ffn_in['router_weight'], 'L0_ffn_router_bias': _L0_ffn_in['router_bias'], 'L0_ffn_expert_bias': _L0_ffn_in['expert_bias']}

def reference(x, ctx_4096, g_xattn, g_ffn, L0_ffn_router_weight, L0_ffn_router_bias, L0_ffn_expert_bias):
    import jax
    import jax.numpy as jnp

    def _L0_xattn_ref(q, k, v):
        import jax, jax.numpy as jnp
        import numpy as np
        EMB_DIM = 128
        HEADS = 8
        B, C, N = q.shape
        H = HEADS
        dh = C // H
        qh = q.transpose(0, 2, 1).reshape(B, N, H, dh)
        kh = k.transpose(0, 2, 1).reshape(B, N, H, dh)
        vh = v.transpose(0, 2, 1).reshape(B, N, H, dh)
        qh = jax.nn.softmax(qh, axis=3)
        kh = jax.nn.softmax(kh, axis=1)
        kvs = jnp.einsum('bnhd,bnhe->bhde', kh, vh)
        out = jnp.einsum('bnhd,bhde->bnhe', qh, kvs)
        return out.transpose(0, 2, 3, 1).reshape(B, C, N)

    def _L0_ffn_ref(hidden_states, router_weight, router_bias, expert_bias):
        import jax, jax.numpy as jnp
        import numpy as np
        K_TOP = 8
        B, S, H = hidden_states.shape
        E = router_weight.shape[0]
        T = B * S
        flat = hidden_states.reshape(T, H)
        logits = jnp.einsum('th,eh->te', flat, router_weight) + router_bias
        scores = jax.nn.softmax(logits, axis=-1)
        topk_w, topk_idx = jax.lax.top_k(scores, K_TOP)
        w_sum = topk_w.sum(axis=-1, keepdims=True)
        w_dense = jnp.zeros((T, E), dtype=scores.dtype).at[jnp.arange(T)[:, None], topk_idx].add(topk_w)
        bias_mix = jnp.einsum('te,eh->th', w_dense, expert_bias)
        out = flat * w_sum + bias_mix
        return out.reshape(B, S, H)
    x = x + jnp.tanh(g_xattn[0]) * _L0_xattn_ref(_layernorm(x, axis=-1), ctx_4096, ctx_4096)
    x = x + jnp.tanh(g_ffn[0]) * _L0_ffn_ref(_layernorm(x, axis=-1), L0_ffn_router_weight, L0_ffn_router_bias, L0_ffn_expert_bias)
    return x

_drawn_inputs = setup_inputs


def setup_inputs(seed=0):
    import zlib

    import numpy as np

    out = dict(_drawn_inputs(seed))
    spreads = {'L0_ffn_router_bias': (0.0, 0.8)}
    factors = {}
    for name, (base, spread) in spreads.items():
        noise = np.random.default_rng([zlib.crc32(name.encode()), seed]).standard_normal(out[name].shape)
        drawn = base * np.exp(spread * noise) if base else spread * noise
        out[name] = jnp.asarray(drawn.astype(out[name].dtype))
    for name, factor in factors.items():
        out[name] = (out[name] * factor).astype(out[name].dtype)
    return out
```

```python
from contextlib import ExitStack

import concourse.bass as bass
from concourse import mybir

F32 = mybir.dt.float32
ALU = mybir.AluOpType
ACT = mybir.ActivationFunctionType
AX_X = mybir.AxisListType.X

P = 128
HEADS = 8
TOP = 8
EPS = 1e-5
HALF = 512
UNROLL = 4
RING = 4


def flamingo_block(nc, x, ctx_in, g_xattn, g_ffn, router_w, router_b, expert_b, out):
    B, C, N = x.shape
    E = router_w.shape[0]
    DH = C // HEADS
    CH = N // P
    HC = HALF // P
    KVN = C + 1
    KVP = C + 4
    AW = C + HEADS
    GROUPS = [(0, 3), (3, 6), (6, 8)]
    FIRST, LOOPS = 1, (B - 3) // UNROLL
    LAST = FIRST + LOOPS * UNROLL
    assert C == P and N == 2 * HALF and CH == 8

    with ExitStack() as stack:
        def sb(name, shape):
            return stack.enter_context(nc.sbuf_tensor(name, shape, F32))

        def bank(name):
            return stack.enter_context(nc.psum_tensor(name, [P, HALF], F32))

        def sem(name):
            return stack.enter_context(nc.semaphore(name))

        x_in = sb("x_in", [P, RING, N])
        c_in = sb("c_in", [P, RING, N])
        x1 = sb("x1", [P, RING, N])
        y = sb("y", [P, 2, N])
        pT = sb("pT", [P, 2, CH, C])
        yT = sb("yT", [P, 2, CH, KVP])
        q = sb("q", [P, 2, N])
        W = sb("W", [P, 2, AW])
        att = sb("att", [P, 2, CH, C])
        x1T = sb("x1T", [P, 2, CH, C])
        wT = sb("wT", [E + 1, 2, C])
        squares = sb("squares", [P, N])
        stats = sb("stats", [P, 2, 2, 6])
        mv = sb("mv", [P, RING, 2])
        ve1 = sb("ve1", [P, RING])
        r1 = sb("r1", [P, RING])
        nb1 = sb("nb1", [P, RING])
        m = sb("m", [P, RING])
        gm = sb("gm", [P, RING])
        rS = sb("rS", [P, 2])
        rG = sb("rG", [P, 2, CH, HEADS])
        rowsum = sb("rowsum", [P, RING, 2])
        nm2 = sb("nm2", [P, RING])
        ssq = sb("ssq", [P, RING])
        ve2 = sb("ve2", [P, RING])
        r2 = sb("r2", [P, RING])
        lg = sb("lg", [P, 2, E])
        nmax = sb("nmax", [P, RING])
        e = sb("e", [P, 2, E])
        tot = sb("tot", [P, RING])
        rtot = sb("rtot", [P, RING])
        score = sb("score", [P, 2, E])
        top8 = sb("top8", [P, 2, TOP])
        rest = sb("rest", [P, 2, E])
        wx = sb("wx", [P, 2, E + 1])
        wsum = sb("wsum", [P, RING])
        rg = sb("rg", [P, RING])
        gain = sb("gain", [P, RING])
        A = sb("A", [P, RING])
        ident = sb("ident", [P, P])
        mask = sb("mask", [P, HEADS, DH])
        maskg = sb("maskg", [P, C])
        half_neg = sb("half_neg", [P, 1])
        gx_raw = sb("gx_raw", [P, 1])
        gf_raw = sb("gf_raw", [P, 1])
        gx = sb("gx", [P, 1])
        gf = sb("gf", [P, 1])
        rb = sb("rb", [P, E])
        rw = sb("rw", [E, N])
        rwc = sb("rwc", [E, N])
        rwT = sb("rwT", [P, CH, E])
        rw_stats = sb("rw_stats", [E, 2, 6])
        rw_mv = sb("rw_mv", [E, 2])
        eb_raw = sb("eb_raw", [E, N])
        eb = sb("eb", [E + 1, N])

        turn = [bank("turn0"), bank("turn1")]
        attp = [bank("attp0"), bank("attp1")]
        acc = [bank("acc0"), bank("acc1")]
        kvp = bank("kvp")
        rout = bank("rout")
        logit_p = rout[:, 0:E]
        wT_p = rout[0:E + 1, E:E + C]

        x_loaded = [sem(f"x_loaded{s}") for s in range(RING)]
        c_loaded = [sem(f"c_loaded{s}") for s in range(RING)]
        stored = [sem(f"stored{s}") for s in range(RING)]
        small_loaded = sem("small_loaded")
        w_loaded = sem("w_loaded")
        zeros_set = sem("zeros_set")
        ident_set = sem("ident_set")
        consts_set = sem("consts_set")
        gates_set = sem("gates_set")
        rw_step = sem("rw_step")
        rw_turned = sem("rw_turned")
        tables_set = sem("tables_set")
        maxed = sem("maxed")
        negated = sem("negated")
        gm_set = sem("gm_set")
        y_turned = sem("y_turned")
        y_taken = sem("y_taken")
        kv_done = sem("kv_done")
        rS_set = sem("rS_set")
        W_set = sem("W_set")
        bn_half = sem("bn_half")
        mv_set = sem("mv_set")
        ve1_set = sem("ve1_set")
        r1_set = sem("r1_set")
        nb1_set = sem("nb1_set")
        q_set = sem("q_set")
        attended = sem("attended")
        rG_set = sem("rG_set")
        divided = sem("divided")
        turned_back = sem("turned_back")
        added = sem("added")
        nm2_set = sem("nm2_set")
        squared = sem("squared")
        ve2_set = sem("ve2_set")
        r2_set = sem("r2_set")
        rg_set = sem("rg_set")
        x1_turned = sem("x1_turned")
        x1T_set = sem("x1T_set")
        logits_done = sem("logits_done")
        lg_set = sem("lg_set")
        nmax_set = sem("nmax_set")
        e_set = sem("e_set")
        rtot_set = sem("rtot_set")
        score_set = sem("score_set")
        top8_set = sem("top8_set")
        rest_set = sem("rest_set")
        kept = sem("kept")
        gain_set = sem("gain_set")
        shift_set = sem("shift_set")
        w_turned = sem("w_turned")
        wT_set = sem("wT_set")
        mixed = sem("mixed")
        finished = sem("finished")

        block = stack.enter_context(nc.Block())

        def steps(eng, step):
            for i in range(-2, FIRST):
                step(i, i, i)
            with eng.Fori(0, LOOPS) as j:
                for k in range(FIRST, FIRST + UNROLL):
                    step(j * UNROLL + k, k, None)
            for i in range(LAST, B + 1):
                step(i, i, i)

        def alone(eng, semaphore, value):
            count = value if isinstance(value, int) else eng.to_reg(value)
            eng.wait_ge(consts_set, 1)
            eng.wait_ge(semaphore, count)

        def has(known, off):
            return known is None or 0 <= known + off < B

        @block.sync
        def _(sp):
            def load(ring, src, t, s, done):
                sp.dma_start(ring[:, s, :], src[t]).then_inc(done[s], 16)

            load(c_in, ctx_in, 0, 0, c_loaded)
            load(x_in, x, 0, 0, x_loaded)
            sp.dma_start(gx_raw[:, :], g_xattn.rearrange("(a b) -> a b", a=1).broadcast_to([P, 1])).then_inc(small_loaded, 16)
            sp.dma_start(gf_raw[:, :], g_ffn.rearrange("(a b) -> a b", a=1).broadcast_to([P, 1])).then_inc(small_loaded, 16)
            sp.dma_start(rb[:, :], router_b.rearrange("(a b) -> a b", a=1).broadcast_to([P, E])).then_inc(small_loaded, 16)
            load(c_in, ctx_in, 1, 1, c_loaded)
            load(x_in, x, 1, 1, x_loaded)
            sp.dma_start(rw[:, :], router_w).then_inc(w_loaded, 16)
            sp.dma_start(eb_raw[:, :], expert_b).then_inc(w_loaded, 16)
            for t in (2, 3):
                load(c_in, ctx_in, t, t, c_loaded)
                load(x_in, x, t, t, x_loaded)
            for s in range(RING):
                sp.sem_inc(stored[s], 16)

            def load_c(t, s):
                sp.wait_ge(negated, t - RING + 1)
                load(c_in, ctx_in, t, s, c_loaded)

            def load_x(t, s):
                sp.wait_ge(added, 2 * (t - RING) + 2)
                load(x_in, x, t, s, x_loaded)

            def store(t, s):
                sp.wait_ge(finished, 2 * t + 6)
                sp.dma_start(out[t], x1[:, s, :]).then_inc(stored[s], 16)

            LOADS = B - 6
            SP_LOOPS = (LOADS - FIRST) // UNROLL
            for i in range(-2, FIRST):
                load_c(i + 6, (i + 6) % RING)
                if i >= 0:
                    load_x(i + 4, i % RING)
            with sp.Fori(0, SP_LOOPS) as j:
                for k in range(FIRST, FIRST + UNROLL):
                    i = j * UNROLL + k
                    load_c(i + 6, (k + 6) % RING)
                    load_x(i + 4, k % RING)
                    store(i - 1, (k - 1) % RING)
            for i in range(FIRST + SP_LOOPS * UNROLL, B + 1):
                if i + 6 < B:
                    load_c(i + 6, (i + 6) % RING)
                if i + 4 < B:
                    load_x(i + 4, i % RING)
                store(i - 1, (i - 1) % RING)
            for s in range(RING):
                sp.wait_ge(stored[s], 16 * (B // RING + 1))

        @block.gpsimd
        def _(pool):
            nc.gpsimd.memset(ident[:, :], 0.0).then_inc(zeros_set, 1)
            nc.gpsimd.memset(mask[:, :, :], 1.0).then_inc(zeros_set, 1)
            nc.gpsimd.memset(W[:, :, C:AW], 1.0).then_inc(zeros_set, 1)
            nc.gpsimd.memset(half_neg[:, :], -0.5).then_inc(zeros_set, 1)
            nc.gpsimd.memset(yT[:, :, :, C:KVN], 1.0).then_inc(zeros_set, 1)
            pool.wait_ge(zeros_set, 5)
            nc.gpsimd.affine_select(out=ident[:, :], in_=ident[:, :], compare_op=ALU.not_equal, fill=1.0,
                                    base=0, pattern=[[-1, P]], channel_multiplier=1).then_inc(ident_set, 1)
            nc.gpsimd.affine_select(out=mask[:, :, :], in_=mask[:, :, :], compare_op=ALU.is_ge, fill=0.0,
                                    base=0, pattern=[[-DH, HEADS], [0, DH]], channel_multiplier=1).then_inc(zeros_set, 1)
            nc.gpsimd.affine_select(out=W[:, :, C:AW], in_=W[:, :, C:AW], compare_op=ALU.is_ge, fill=0.0,
                                    base=0, pattern=[[0, 2], [-DH, HEADS]], channel_multiplier=1).then_inc(zeros_set, 1)
            pool.wait_ge(zeros_set, 7)
            nc.gpsimd.affine_select(out=mask[:, :, :], in_=mask[:, :, :], compare_op=ALU.is_ge, fill=0.0,
                                    base=DH - 1, pattern=[[DH, HEADS], [0, DH]], channel_multiplier=-1).then_inc(zeros_set, 1)
            nc.gpsimd.affine_select(out=W[:, :, C:AW], in_=W[:, :, C:AW], compare_op=ALU.is_ge, fill=0.0,
                                    base=DH - 1, pattern=[[0, 2], [DH, HEADS]], channel_multiplier=-1).then_inc(zeros_set, 1)
            pool.wait_ge(zeros_set, 9)
            nc.gpsimd.tensor_copy(mask[0:1, 0:1, 0:1], mask[0:1, 0:1, 0:1]).then_inc(consts_set, 1)

            def negate(t, s):
                alone(pool, maxed, t + 1)
                nc.gpsimd.tensor_scalar(y[:, s % 2, :], c_in[:, s, :], -1.0, m[:, s:s + 1],
                                        ALU.mult, ALU.add).then_inc(negated, 1)
                nc.gpsimd.tensor_scalar(gm[:, s:s + 1], m[:, s:s + 1], gx[:, 0:1], 1.0,
                                        ALU.mult, ALU.mult).then_inc(gm_set, 1)

            def x_scale(t, s):
                alone(pool, mv_set, t + 1)
                nc.gpsimd.tensor_scalar(ve1[:, s:s + 1], mv[:, s, 1:2], 1.0, EPS,
                                        ALU.mult, ALU.add).then_inc(ve1_set, 1)
                alone(pool, ve1_set, t + 1)
                nc.gpsimd.tensor_tensor(r1[:, s:s + 1], ve1[:, s:s + 1], half_neg[:, :], ALU.pow).then_inc(r1_set, 1)
                alone(pool, r1_set, t + 1)
                nc.gpsimd.tensor_scalar(nb1[:, s:s + 1], mv[:, s, 0:1], r1[:, s:s + 1], -1.0,
                                        ALU.mult, ALU.mult).then_inc(nb1_set, 1)

            def x1_mean(t, s):
                alone(pool, added, 2 * t + 2)
                nc.gpsimd.tensor_scalar(nm2[:, s:s + 1], rowsum[:, s, 0:1], rowsum[:, s, 1:2], -1.0 / N,
                                        ALU.add, ALU.mult).then_inc(nm2_set, 1)

            def x1_scale(t, s):
                alone(pool, squared, t + 1)
                nc.gpsimd.tensor_scalar(ve2[:, s:s + 1], ssq[:, s:s + 1], 1.0 / N, EPS,
                                        ALU.mult, ALU.add).then_inc(ve2_set, 1)
                alone(pool, ve2_set, t + 1)
                nc.gpsimd.tensor_tensor(r2[:, s:s + 1], ve2[:, s:s + 1], half_neg[:, :], ALU.pow).then_inc(r2_set, 1)
                alone(pool, r2_set, t + 1)
                nc.gpsimd.tensor_scalar(rg[:, s:s + 1], r2[:, s:s + 1], gf[:, 0:1], 1.0,
                                        ALU.mult, ALU.mult).then_inc(rg_set, 1)

            def gains(t, s):
                alone(pool, kept, t + 1)
                pool.wait_ge(rg_set, t + 1)
                nc.gpsimd.tensor_scalar(gain[:, s:s + 1], wsum[:, s:s + 1], rg[:, s:s + 1], 1.0,
                                        ALU.mult, ALU.mult).then_inc(gain_set, 1)
                alone(pool, gain_set, t + 1)
                nc.gpsimd.tensor_scalar(wx[:, s % 2, E:E + 1], gain[:, s:s + 1], nm2[:, s:s + 1], 1.0,
                                        ALU.mult, ALU.mult).then_inc(shift_set, 1)
                nc.gpsimd.tensor_scalar(A[:, s:s + 1], gain[:, s:s + 1], 1.0, 1.0,
                                        ALU.mult, ALU.add).then_inc(shift_set, 1)

            pool.wait_ge(gates_set, 2)

            def step(i, k, known):
                if has(known, -1):
                    x1_scale(i - 1, (k - 1) % RING)
                if has(known, 2):
                    if known is None or known >= 0:
                        alone(pool, y_turned, 2 * i + 2)
                    negate(i + 2, (k + 2) % RING)
                if has(known, -1):
                    gains(i - 1, (k - 1) % RING)
                if has(known, 0):
                    x1_mean(i, k % RING)
                if has(known, 2):
                    x_scale(i + 2, (k + 2) % RING)

            steps(pool, step)

        @block.scalar
        def _(act):
            act.wait_ge(small_loaded, 48)
            nc.scalar.activation(gx[:, :], gx_raw[:, :], ACT.Tanh).then_inc(gates_set, 1)
            nc.scalar.activation(gf[:, :], gf_raw[:, :], ACT.Tanh).then_inc(gates_set, 1)

            def query(t, s):
                act.wait_ge(nb1_set, t + 1)
                nc.scalar.activation(q[:, s % 2, :], x_in[:, s, :], ACT.Exp, bias=nb1[:, s:s + 1],
                                     scale=r1[:, s:s + 1]).then_inc(q_set, 1)

            def expert_exp(t, s):
                act.wait_ge(nmax_set, t + 1)
                nc.scalar.activation(e[:, s % 2, :], lg[:, s % 2, :], ACT.Exp, bias=nmax[:, s:s + 1],
                                     accum_out=tot[:, s:s + 1]).then_inc(e_set, 1)

            def take_x1(t, s):
                for h in range(2):
                    act.wait_ge(x1_turned, 2 * t + h + 1)
                    nc.scalar.copy(x1T[:, s % 2, HC * h:HC * h + HC, :],
                                   turn[h][:, :].rearrange("p (c n) -> p c n", c=HC)).then_inc(x1T_set, 1)

            def take_w(t, s):
                act.wait_ge(w_turned, t + 1)
                nc.scalar.copy(wT[:, s % 2, :], wT_p).then_inc(wT_set, 1)

            def take_y(t, s):
                for h in range(2):
                    src = turn[h][:, :].rearrange("p (c n) -> p c n", c=HC)
                    act.wait_ge(y_turned, 2 * t + h + 1)
                    nc.scalar.activation(pT[:, s % 2, HC * h:HC * h + HC, :], src, ACT.Exp,
                                         scale=-1.0).then_inc(y_taken, 1)
                    nc.scalar.copy(yT[:, s % 2, HC * h:HC * h + HC, 0:C], src).then_inc(y_taken, 1)

            def square(t, s):
                act.wait_ge(nm2_set, t + 1)
                nc.scalar.activation(squares[:, :], x1[:, s, :], ACT.Square, bias=nm2[:, s:s + 1],
                                     accum_out=ssq[:, s:s + 1]).then_inc(squared, 1)

            def step(i, k, known):
                if has(known, 1):
                    if known is None or known >= 1:
                        act.wait_ge(attended, 3 * i)
                    query(i + 1, (k + 1) % RING)
                if has(known, -1):
                    expert_exp(i - 1, (k - 1) % RING)
                if has(known, 0):
                    take_x1(i, k % RING)
                if has(known, -1):
                    take_w(i - 1, (k - 1) % RING)
                if has(known, 2):
                    if known is None or known >= 0:
                        act.wait_ge(kv_done, i + 1)
                    take_y(i + 2, (k + 2) % RING)
                if has(known, 0):
                    square(i, k % RING)

            steps(act, step)

        @block.vector
        def _(dve):
            dve.wait_ge(consts_set, 1)
            dve.wait_ge(gates_set, 2)
            nc.vector.memset(eb[E:E + 1, :], 1.0).then_inc(tables_set, 1)
            nc.vector.tensor_scalar(maskg[:, :], mask[:, :, :].rearrange("p h d -> p (h d)"), gx[:, 0:1], -1.0,
                                    ALU.mult, ALU.mult).then_inc(tables_set, 1)
            nc.vector.memset(rest[:, 0, 0:1], 0.0).then_inc(finished, 4)

            def router_tables():
                dve.wait_ge(w_loaded, 32)
                for h in range(2):
                    nc.vector.bn_stats(rw_stats[:, h, :], rw[:, HALF * h:HALF * h + HALF]).then_inc(rw_step, 1)
                dve.wait_ge(rw_step, 2)
                nc.vector.bn_aggr(rw_mv[:, :], rw_stats[:, :, :]).then_inc(rw_step, 1)
                dve.wait_ge(rw_step, 3)
                nc.vector.tensor_scalar(rwc[:, :], rw[:, :], rw_mv[:, 0:1], None, ALU.subtract).then_inc(rw_step, 1)
                nc.vector.tensor_scalar(eb[0:E, :], eb_raw[:, :], gf[0:E, 0:1], None, ALU.mult).then_inc(tables_set, 1)
                dve.wait_ge(rw_turned, 1)
                nc.vector.tensor_copy(rwT[:, :, :], attp[0][:, 0:CH * E].rearrange("p (c e) -> p c e", c=CH)
                                      ).then_inc(tables_set, 1)

            def divide(t, s, g):
                a, b = GROUPS[g]
                src = attp[g % 2][:, 0:(b - a) * AW].rearrange("p (c w) -> p c w", c=b - a)
                dve.wait_ge(attended, 3 * t + g + 1)
                nc.vector.reciprocal(rG[:, s % 2, a:b, :], src[:, :, C:AW]).then_inc(rG_set, 1)
                dve.wait_ge(rG_set, 3 * t + g + 1)
                nc.vector.tensor_tensor(att[:, s % 2, a:b, :].rearrange("p c (h d) -> p c h d", h=HEADS),
                                        src[:, :, 0:C].rearrange("p c (h d) -> p c h d", h=HEADS),
                                        rG[:, s % 2, a:b, :].unsqueeze(3).broadcast_to([P, b - a, HEADS, DH]),
                                        ALU.mult).then_inc(divided, 1)

            def add(t, s, h):
                cols = slice(HALF * h, HALF * h + HALF)
                if h == 0:
                    dve.wait_ge(stored[s], load_count(t, s))
                    dve.wait_ge(gm_set, t + 1)
                dve.wait_ge(turned_back, 2 * t + h + 1)
                nc.vector.scalar_tensor_tensor(out=x1[:, s, cols], in0=x_in[:, s, cols], scalar=gm[:, s:s + 1],
                                               in1=acc[h][:, :], op0=ALU.add, op1=ALU.add,
                                               accum_out=rowsum[:, s, h:h + 1]).then_inc(added, 1)

            def final(t, s):
                for h in range(2):
                    cols = slice(HALF * h, HALF * h + HALF)
                    dve.wait_ge(mixed, 2 * t + h + 1)
                    if h == 0:
                        dve.wait_ge(squared, t + 1)
                    nc.vector.scalar_tensor_tensor(out=x1[:, s, cols], in0=x1[:, s, cols], scalar=A[:, s:s + 1],
                                                   in1=acc[h][:, :], op0=ALU.mult, op1=ALU.add).then_inc(finished, 1)

            def x_stats(t, s, h):
                if h == 0:
                    dve.wait_ge(x_loaded[s], load_count(t, s))
                nc.vector.bn_stats(stats[:, s % 2, h, :], x_in[:, s, HALF * h:HALF * h + HALF]).then_inc(bn_half, 1)

            def x_mean(t, s):
                alone(dve, bn_half, 2 * t + 2)
                nc.vector.bn_aggr(mv[:, s, :], stats[:, s % 2, :, :]).then_inc(mv_set, 1)

            def load_count(t, s):
                return (t - s) * (16 // RING) + 16

            def ctx_max(t, s):
                dve.wait_ge(c_loaded[s], load_count(t, s))
                nc.vector.tensor_reduce(m[:, s:s + 1], c_in[:, s, :], AX_X, ALU.max).then_inc(maxed, 1)

            def weights(t, s):
                dve.wait_ge(kv_done, t + 1)
                nc.vector.reciprocal(rS[:, s % 2:s % 2 + 1], kvp[:, C:KVN]).then_inc(rS_set, 1)
                dve.wait_ge(rS_set, t + 1)
                nc.vector.scalar_tensor_tensor(out=W[:, s % 2, 0:C], in0=kvp[:, 0:C], scalar=rS[:, s % 2:s % 2 + 1],
                                               in1=maskg[:, :], op0=ALU.mult, op1=ALU.mult).then_inc(W_set, 1)

            def logits(t, s):
                dve.wait_ge(logits_done, t + 1)
                dve.wait_ge(r2_set, t + 1)
                nc.vector.scalar_tensor_tensor(out=lg[:, s % 2, :], in0=logit_p, scalar=r2[:, s:s + 1],
                                               in1=rb[:, :], op0=ALU.mult, op1=ALU.add).then_inc(lg_set, 1)

            def logit_max(t, s):
                dve.wait_ge(lg_set, t + 1)
                nc.vector.tensor_reduce(nmax[:, s:s + 1], lg[:, s % 2, :], AX_X, ALU.max,
                                        negate=True).then_inc(nmax_set, 1)

            def scores(t, s):
                dve.wait_ge(e_set, t + 1)
                nc.vector.reciprocal(rtot[:, s:s + 1], tot[:, s:s + 1]).then_inc(rtot_set, 1)
                dve.wait_ge(rtot_set, t + 1)
                nc.vector.tensor_scalar(score[:, s % 2, :], e[:, s % 2, :], rtot[:, s:s + 1], None,
                                        ALU.mult).then_inc(score_set, 1)

            def keep_top(t, s):
                alone(dve, score_set, t + 1)
                nc.vector.max(top8[:, s % 2, :], score[:, s % 2, :]).then_inc(top8_set, 1)
                alone(dve, top8_set, t + 1)
                nc.vector.match_replace(rest[:, s % 2, :], top8[:, s % 2, :], score[:, s % 2, :], 0.0).then_inc(rest_set, 1)
                dve.wait_ge(rest_set, t + 1)
                nc.vector.scalar_tensor_tensor(out=wx[:, s % 2, 0:E], in0=score[:, s % 2, :], scalar=1.0,
                                               in1=rest[:, s % 2, :], op0=ALU.mult, op1=ALU.subtract,
                                               accum_out=wsum[:, s:s + 1]).then_inc(kept, 1)

            def step(i, k, known):
                a, b, c, n = (k + 2) % RING, k % RING, (k - 1) % RING, (k + 1) % RING
                if has(known, 0):
                    divide(i, b, 0)
                    divide(i, b, 1)
                    divide(i, b, 2)
                if has(known, -1):
                    logits(i - 1, c)
                    logit_max(i - 1, c)
                if has(known, 2):
                    ctx_max(i + 2, a)
                if has(known, 0):
                    add(i, b, 0)
                if has(known, -1):
                    scores(i - 1, c)
                if has(known, 0):
                    add(i, b, 1)
                if has(known, -1):
                    keep_top(i - 1, c)
                if has(known, 1):
                    weights(i + 1, n)
                if has(known, 2):
                    x_stats(i + 2, a, 0)
                    x_stats(i + 2, a, 1)
                    x_mean(i + 2, a)
                if known == -1:
                    router_tables()
                if has(known, -1):
                    final(i - 1, c)

            steps(dve, step)

        @block.tensor
        def _(pe):
            pe.wait_ge(ident_set, 1)

            def turn_y(t, s):
                pe.wait_ge(negated, t + 1)
                for h in range(2):
                    for j in range(HC):
                        col = HALF * h + P * j
                        last = nc.tensor.transpose(turn[h][:, P * j:P * j + P], y[:, s % 2, col:col + P], ident[:, :])
                    last.then_inc(y_turned, 1)

            def kvs(t, s):
                pe.wait_ge(y_taken, 4 * t + 4)
                for ch in range(CH):
                    last = nc.tensor.matmul(kvp[:, 0:KVN], pT[:, s % 2, ch, :], yT[:, s % 2, ch, 0:KVN],
                                            start=(ch == 0), stop=(ch == CH - 1))
                last.then_inc(kv_done, 1)

            def attend(t, s, g):
                a, b = GROUPS[g]
                for ch in range(a, b):
                    o = (ch - a) * AW
                    last = nc.tensor.matmul(attp[g % 2][:, o:o + AW], q[:, s % 2, P * ch:P * ch + P],
                                            W[:, s % 2, :], start=True, stop=True)
                last.then_inc(attended, 1)

            def turn_back(t, s):
                for h in range(2):
                    pe.wait_ge(finished, 2 * t + h + 1)
                    pe.wait_ge(divided, 3 * t + 2 + h)
                    for j in range(HC):
                        last = nc.tensor.transpose(acc[h][:, P * j:P * j + P], att[:, s % 2, HC * h + j, :], ident[:, :])
                    last.then_inc(turned_back, 1)

            def turn_x1(t, s):
                for h in range(2):
                    pe.wait_ge(added, 2 * t + h + 1)
                    for j in range(HC):
                        col = HALF * h + P * j
                        last = nc.tensor.transpose(turn[h][:, P * j:P * j + P], x1[:, s, col:col + P], ident[:, :])
                    last.then_inc(x1_turned, 1)

            def route(t, s):
                for ch in range(CH):
                    if ch % HC == 0:
                        pe.wait_ge(x1T_set, 2 * t + ch // HC + 1)
                    last = nc.tensor.matmul(logit_p, x1T[:, s % 2, ch, :], rwT[:, ch, :],
                                            start=(ch == 0), stop=(ch == CH - 1))
                last.then_inc(logits_done, 1)

            def turn_w(t, s):
                pe.wait_ge(kept, t + 1)
                pe.wait_ge(shift_set, 2 * t + 2)
                nc.tensor.transpose(wT_p, wx[:, s % 2, :], ident[:, :]).then_inc(w_turned, 1)

            def mix(t, s):
                pe.wait_ge(wT_set, t + 1)
                for h in range(2):
                    nc.tensor.matmul(acc[h][:, :], wT[:, s % 2, :], eb[:, HALF * h:HALF * h + HALF],
                                     start=True, stop=True).then_inc(mixed, 1)

            def step(i, k, known):
                a, b, c, n = (k + 2) % RING, k % RING, (k - 1) % RING, (k + 1) % RING
                if has(known, 0):
                    pe.wait_ge(divided, 3 * i + 1)
                    attend(i, b, 2)
                    turn_back(i, b)
                if has(known, 1):
                    if known is None or known >= 0:
                        pe.wait_ge(W_set, i + 1)
                    kvs(i + 1, n)
                if known == -1:
                    pe.wait_ge(rw_step, 4)
                    for ch in range(CH):
                        last = nc.tensor.transpose(attp[0][:, E * ch:E * ch + E], rwc[:, P * ch:P * ch + P],
                                                   ident[0:E, 0:E])
                    last.then_inc(rw_turned, 1)
                if has(known, 0):
                    if known is None or known + 1 < B:
                        pe.wait_ge(y_taken, 4 * i + 8)
                    turn_x1(i, b)
                if has(known, -1):
                    turn_w(i - 1, c)
                if has(known, -1):
                    if has(known, 0):
                        pe.wait_ge(added, 2 * i + 2)
                    mix(i - 1, c)
                if has(known, 2):
                    if has(known, 0):
                        pe.wait_ge(x1T_set, 2 * i + 2)
                    elif known == -1:
                        pe.wait_ge(y_taken, 4)
                    turn_y(i + 2, a)
                if has(known, 0):
                    if known is None or known >= 1:
                        pe.wait_ge(wT_set, i)
                    if known == 0:
                        pe.wait_ge(tables_set, 4)
                    route(i, b)
                if has(known, 1):
                    if known == -1:
                        pe.wait_ge(tables_set, 4)
                    else:
                        pe.wait_ge(divided, 3 * i + 3)
                    pe.wait_ge(q_set, i + 2)
                    pe.wait_ge(W_set, i + 2)
                    attend(i + 1, n, 0)
                    attend(i + 1, n, 1)

            steps(pe, step)


_INS = ['x', 'ctx_4096', 'g_xattn', 'g_ffn', 'L0_ffn_router_weight', 'L0_ffn_router_bias', 'L0_ffn_expert_bias']
_OUT = ((16, 128, 1024), 'float32')


def kernel(**inputs):
    import numpy as _np
    import concourse.bacc as _bacc
    from concourse import mybir as _mybir
    from concourse.bass_utils import run_bass_kernel_spmd as _run

    nc = _bacc.Bacc("TRN2", target_bir_lowering=False, num_devices=1)
    arrays, args = {}, []
    for name in _INS:
        a = _np.ascontiguousarray(inputs[name])
        arrays[f"in_{name}_dram"] = a
        args.append(nc.dram_tensor(f"in_{name}_dram", a.shape, _mybir.dt.from_np(a.dtype), kind="ExternalInput").ap())
    shape, dtype = _OUT
    args.append(nc.dram_tensor("out_dram", shape, _mybir.dt.from_np(_np.dtype(dtype)), kind="ExternalOutput").ap())
    flamingo_block(nc, *args)
    r = _run(nc, [arrays], core_ids=[0])
    return r.results[0]["out_dram"]
```

```python
from contextlib import ExitStack

import concourse.bass as bass
from concourse import mybir

F32 = mybir.dt.float32
ALU = mybir.AluOpType
ACT = mybir.ActivationFunctionType
AX_X = mybir.AxisListType.X

P = 128
HEADS = 8
TOP = 8
EPS = 1e-5
HALF = 512
UNROLL = 4
RING = 4


def flamingo_block(nc, x, ctx_in, g_xattn, g_ffn, router_w, router_b, expert_b, out):
    B, C, N = x.shape
    E = router_w.shape[0]
    DH = C // HEADS
    CH = N // P
    HC = HALF // P
    CT = 32
    TILES = C // CT
    KVN = CT + 1
    AW = C + HEADS
    GROUPS = [(0, 3), (3, 6), (6, 8)]
    ROOT = float(N) ** 0.5
    FIRST, LOOPS = 2, (B - 5) // UNROLL
    LAST = FIRST + LOOPS * UNROLL
    assert C == P and N == 2 * HALF and CH == 8

    with ExitStack() as stack:
        def sb(name, shape):
            return stack.enter_context(nc.sbuf_tensor(name, shape, F32))

        def bank(name):
            return stack.enter_context(nc.psum_tensor(name, [P, HALF], F32))

        def sem(name):
            return stack.enter_context(nc.semaphore(name))

        x_in = sb("x_in", [P, RING, N])
        c_in = sb("c_in", [P, RING, N])
        x1 = sb("x1", [P, RING, N])
        y = sb("y", [P, 2, N])
        pT = sb("pT", [P, 2, CH, C])
        yT = sb("yT", [P, 2, CH, TILES, KVN])
        q = sb("q", [P, 2, N])
        W = sb("W", [P, 2, AW])
        att = sb("att", [P, 2, CH, C])
        x1T = sb("x1T", [P, 2, CH, C])
        wT = sb("wT", [E, 2, C])
        x_copy = sb("x_copy", [P, N])
        x_squares = sb("x_squares", [P, N])
        squares = sb("squares", [P, N])
        xsum = sb("xsum", [P, RING])
        nm1 = sb("nm1", [P, RING])
        var1 = sb("var1", [P, RING])
        ve1 = sb("ve1", [P, RING])
        r1 = sb("r1", [P, RING])
        nb1 = sb("nb1", [P, RING])
        m = sb("m", [P, RING])
        gm = sb("gm", [P, RING])
        rS = sb("rS", [P, 2])
        rG = sb("rG", [P, 2, CH, HEADS])
        rowsum = sb("rowsum", [P, RING, 2])
        nm2 = sb("nm2", [P, RING])
        var2 = sb("var2", [P, RING])
        ve2 = sb("ve2", [P, RING])
        r2 = sb("r2", [P, RING])
        parts = sb("parts", [2 * E, C])
        lg = sb("lg", [P, 2, E])
        nmax = sb("nmax", [P, RING])
        e = sb("e", [P, 2, E])
        tot = sb("tot", [P, RING])
        rtot = sb("rtot", [P, RING])
        score = sb("score", [P, 2, E])
        top8 = sb("top8", [P, 2, TOP])
        rest = sb("rest", [P, 2, E])
        wx = sb("wx", [P, 2, E])
        wsum = sb("wsum", [P, RING])
        gain = sb("gain", [P, RING])
        A = sb("A", [P, RING])
        shift = sb("shift", [P, RING])
        ident = sb("ident", [P, P])
        fold = sb("fold", [2 * E, E])
        mask = sb("mask", [P, HEADS, DH])
        maskg = sb("maskg", [P, C])
        half_neg = sb("half_neg", [P, 1])
        gx_raw = sb("gx_raw", [P, 1])
        gf_raw = sb("gf_raw", [P, 1])
        gx = sb("gx", [P, 1])
        gf = sb("gf", [P, 1])
        rb = sb("rb", [P, E])
        rw = sb("rw", [E, N])
        rwc = sb("rwc", [E, N])
        rwT = sb("rwT", [P, CH, E])
        rw_stats = sb("rw_stats", [E, 2, 6])
        rw_mv = sb("rw_mv", [E, 2])
        eb_raw = sb("eb_raw", [E, N])
        eb = sb("eb", [E, N])

        turn = [bank("turn0"), bank("turn1")]
        attp = [bank("attp0"), bank("attp1")]
        back = [bank("back0"), bank("back1")]
        mixp = [back[0], bank("mix1")]
        small = bank("small")
        kvp = small[:, 0:KVN]
        wT_p = small[0:E, E:E + C]
        parts_p = small[:, E + C:E + 2 * C]
        logit_p = small[:, E + 2 * C:2 * E + 2 * C]

        x_loaded = [sem(f"x_loaded{s}") for s in range(RING)]
        c_loaded = [sem(f"c_loaded{s}") for s in range(RING)]
        stored = [sem(f"stored{s}") for s in range(RING)]
        small_loaded = sem("small_loaded")
        w_loaded = sem("w_loaded")
        zeros_set = sem("zeros_set")
        ident_set = sem("ident_set")
        consts_set = sem("consts_set")
        gates_set = sem("gates_set")
        rw_step = sem("rw_step")
        rw_turned = sem("rw_turned")
        tables_set = sem("tables_set")
        maxed = sem("maxed")
        negated = sem("negated")
        gm_set = sem("gm_set")
        y_turned = sem("y_turned")
        y_taken = sem("y_taken")
        kv_done = sem("kv_done")
        rS_set = sem("rS_set")
        W_set = sem("W_set")
        x_summed = sem("x_summed")
        nm1_set = sem("nm1_set")
        x_squared = sem("x_squared")
        ve1_set = sem("ve1_set")
        r1_set = sem("r1_set")
        nb1_set = sem("nb1_set")
        q_set = sem("q_set")
        attended = sem("attended")
        rG_set = sem("rG_set")
        divided = sem("divided")
        turned_back = sem("turned_back")
        added = sem("added")
        nm2_set = sem("nm2_set")
        squared = sem("squared")
        ve2_set = sem("ve2_set")
        r2_set = sem("r2_set")
        x1_turned = sem("x1_turned")
        x1T_set = sem("x1T_set")
        parts_done = sem("parts_done")
        parts_set = sem("parts_set")
        logits_done = sem("logits_done")
        lg_set = sem("lg_set")
        nmax_set = sem("nmax_set")
        e_set = sem("e_set")
        rtot_set = sem("rtot_set")
        score_set = sem("score_set")
        top8_set = sem("top8_set")
        rest_set = sem("rest_set")
        kept = sem("kept")
        gain_set = sem("gain_set")
        shift_set = sem("shift_set")
        rescaled = sem("rescaled")
        w_turned = sem("w_turned")
        wT_set = sem("wT_set")
        mixed = sem("mixed")
        finished = sem("finished")

        block = stack.enter_context(nc.Block())

        def steps(eng, step):
            for i in range(-3, FIRST):
                step(i, i, i)
            with eng.Fori(0, LOOPS) as j:
                for k in range(FIRST, FIRST + UNROLL):
                    step(j * UNROLL + k, k, None)
            for i in range(LAST, B + 2):
                step(i, i, i)

        def alone(eng, semaphore, value):
            count = value if isinstance(value, int) else eng.to_reg(value)
            eng.wait_ge(consts_set, 1)
            eng.wait_ge(semaphore, count)

        def load_count(t, s):
            return (t - s) * (16 // RING) + 16

        def has(known, off):
            return known is None or 0 <= known + off < B

        @block.sync
        def _(sp):
            def load(ring, src, t, s, done):
                sp.dma_start(ring[:, s, :], src[t]).then_inc(done[s], 16)

            load(c_in, ctx_in, 0, 0, c_loaded)
            load(x_in, x, 0, 0, x_loaded)
            sp.dma_start(gx_raw[:, :], g_xattn.rearrange("(a b) -> a b", a=1).broadcast_to([P, 1])).then_inc(small_loaded, 16)
            sp.dma_start(gf_raw[:, :], g_ffn.rearrange("(a b) -> a b", a=1).broadcast_to([P, 1])).then_inc(small_loaded, 16)
            sp.dma_start(rb[:, :], router_b.rearrange("(a b) -> a b", a=1).broadcast_to([P, E])).then_inc(small_loaded, 16)
            load(c_in, ctx_in, 1, 1, c_loaded)
            load(x_in, x, 1, 1, x_loaded)
            sp.dma_start(rw[:, :], router_w).then_inc(w_loaded, 16)
            sp.dma_start(eb_raw[:, :], expert_b).then_inc(w_loaded, 16)
            for t in (2, 3):
                load(c_in, ctx_in, t, t, c_loaded)
                load(x_in, x, t, t, x_loaded)
            for s in range(RING):
                sp.sem_inc(stored[s], 16)

            def load_c(t, s):
                sp.wait_ge(negated, t - RING + 1)
                load(c_in, ctx_in, t, s, c_loaded)

            def load_x(t, s):
                sp.wait_ge(added, 2 * (t - RING) + 2)
                load(x_in, x, t, s, x_loaded)

            def store(t, s):
                sp.wait_ge(finished, 2 * t + 2)
                sp.dma_start(out[t], x1[:, s, :]).then_inc(stored[s], 16)

            SP_LOOPS = (B - 7 - FIRST) // UNROLL
            for i in range(-3, FIRST):
                if i >= 0:
                    load_x(i + 4, i % RING)
                load_c(i + 7, (i + 7) % RING)
            with sp.Fori(0, SP_LOOPS) as j:
                for k in range(FIRST, FIRST + UNROLL):
                    i = j * UNROLL + k
                    store(i - 2, (k - 2) % RING)
                    load_x(i + 4, k % RING)
                    load_c(i + 7, (k + 7) % RING)
            for i in range(FIRST + SP_LOOPS * UNROLL, B + 2):
                store(i - 2, (i - 2) % RING)
                if i + 4 < B:
                    load_x(i + 4, i % RING)
                if i + 7 < B:
                    load_c(i + 7, (i + 7) % RING)
            for s in range(RING):
                sp.wait_ge(stored[s], 16 * (B // RING + 1))

        @block.gpsimd
        def _(pool):
            nc.gpsimd.memset(ident[:, :], 0.0).then_inc(zeros_set, 1)
            nc.gpsimd.memset(mask[:, :, :], 1.0).then_inc(zeros_set, 1)
            nc.gpsimd.memset(W[:, :, C:AW], 1.0).then_inc(zeros_set, 1)
            nc.gpsimd.memset(half_neg[:, :], -0.5).then_inc(zeros_set, 1)
            nc.gpsimd.memset(yT[:, :, :, :, CT:KVN], 1.0).then_inc(zeros_set, 1)
            nc.gpsimd.memset(fold[:, :], 0.0).then_inc(zeros_set, 1)
            pool.wait_ge(zeros_set, 6)
            nc.gpsimd.affine_select(out=ident[:, :], in_=ident[:, :], compare_op=ALU.not_equal, fill=1.0,
                                    base=0, pattern=[[-1, P]], channel_multiplier=1).then_inc(ident_set, 1)
            nc.gpsimd.affine_select(out=mask[:, :, :], in_=mask[:, :, :], compare_op=ALU.is_ge, fill=0.0,
                                    base=0, pattern=[[-DH, HEADS], [0, DH]], channel_multiplier=1).then_inc(zeros_set, 1)
            nc.gpsimd.affine_select(out=W[:, :, C:AW], in_=W[:, :, C:AW], compare_op=ALU.is_ge, fill=0.0,
                                    base=0, pattern=[[0, 2], [-DH, HEADS]], channel_multiplier=1).then_inc(zeros_set, 1)
            nc.gpsimd.affine_select(out=fold[:, :], in_=fold[:, :], compare_op=ALU.not_equal, fill=1.0,
                                    base=0, pattern=[[-1, E]], channel_multiplier=1).then_inc(zeros_set, 1)
            pool.wait_ge(zeros_set, 9)
            nc.gpsimd.affine_select(out=mask[:, :, :], in_=mask[:, :, :], compare_op=ALU.is_ge, fill=0.0,
                                    base=DH - 1, pattern=[[DH, HEADS], [0, DH]], channel_multiplier=-1).then_inc(zeros_set, 1)
            nc.gpsimd.affine_select(out=W[:, :, C:AW], in_=W[:, :, C:AW], compare_op=ALU.is_ge, fill=0.0,
                                    base=DH - 1, pattern=[[0, 2], [DH, HEADS]], channel_multiplier=-1).then_inc(zeros_set, 1)
            nc.gpsimd.affine_select(out=fold[:, :], in_=fold[:, :], compare_op=ALU.not_equal, fill=1.0,
                                    base=-E, pattern=[[-1, E]], channel_multiplier=1).then_inc(zeros_set, 1)
            pool.wait_ge(zeros_set, 12)
            nc.gpsimd.tensor_copy(mask[0:1, 0:1, 0:1], mask[0:1, 0:1, 0:1]).then_inc(consts_set, 1)

            def negate(t, s):
                alone(pool, maxed, t + 1)
                nc.gpsimd.tensor_scalar(y[:, s % 2, :], c_in[:, s, :], -1.0, m[:, s:s + 1],
                                        ALU.mult, ALU.add).then_inc(negated, 1)

            def gated_max(t, s):
                nc.gpsimd.tensor_scalar(gm[:, s:s + 1], m[:, s:s + 1], gx[:, 0:1], 1.0,
                                        ALU.mult, ALU.mult).then_inc(gm_set, 1)

            def x_mean(t, s):
                alone(pool, x_summed, t + 1)
                nc.gpsimd.tensor_scalar(nm1[:, s:s + 1], xsum[:, s:s + 1], -1.0 / (N * ROOT), 0.0,
                                        ALU.mult, ALU.add).then_inc(nm1_set, 1)

            def x_scale(t, s):
                alone(pool, x_squared, t + 1)
                nc.gpsimd.tensor_scalar(ve1[:, s:s + 1], var1[:, s:s + 1], EPS, 1.0,
                                        ALU.add, ALU.mult).then_inc(ve1_set, 1)
                alone(pool, ve1_set, t + 1)
                nc.gpsimd.tensor_tensor(r1[:, s:s + 1], ve1[:, s:s + 1], half_neg[:, :], ALU.pow).then_inc(r1_set, 1)
                alone(pool, r1_set, t + 1)
                nc.gpsimd.tensor_scalar(nb1[:, s:s + 1], nm1[:, s:s + 1], r1[:, s:s + 1], ROOT,
                                        ALU.mult, ALU.mult).then_inc(nb1_set, 1)

            def x1_mean(t, s):
                alone(pool, added, 2 * t + 2)
                nc.gpsimd.tensor_scalar(nm2[:, s:s + 1], rowsum[:, s, 0:1], rowsum[:, s, 1:2], -1.0 / (N * ROOT),
                                        ALU.add, ALU.mult).then_inc(nm2_set, 1)

            def x1_scale(t, s):
                alone(pool, squared, t + 1)
                nc.gpsimd.tensor_scalar(ve2[:, s:s + 1], var2[:, s:s + 1], EPS, 1.0,
                                        ALU.add, ALU.mult).then_inc(ve2_set, 1)
                alone(pool, ve2_set, t + 1)
                nc.gpsimd.tensor_tensor(r2[:, s:s + 1], ve2[:, s:s + 1], half_neg[:, :], ALU.pow).then_inc(r2_set, 1)

            def gains(t, s):
                alone(pool, kept, t + 1)
                nc.gpsimd.tensor_scalar(gain[:, s:s + 1], wsum[:, s:s + 1], r2[:, s:s + 1], gf[:, 0:1],
                                        ALU.mult, ALU.mult).then_inc(gain_set, 1)
                alone(pool, gain_set, t + 1)
                nc.gpsimd.tensor_scalar(shift[:, s:s + 1], nm2[:, s:s + 1], gain[:, s:s + 1], ROOT,
                                        ALU.mult, ALU.mult).then_inc(shift_set, 1)
                nc.gpsimd.tensor_scalar(A[:, s:s + 1], gain[:, s:s + 1], 1.0, 1.0,
                                        ALU.mult, ALU.add).then_inc(shift_set, 1)

            def rescale(t, s):
                alone(pool, shift_set, 2 * t + 2)
                pool.wait_ge(squared, t + 1)
                pool.wait_ge(x1_turned, 2 * t + 2)
                nc.gpsimd.tensor_scalar(x1[:, s, :], x1[:, s, :], A[:, s:s + 1], shift[:, s:s + 1],
                                        ALU.mult, ALU.add).then_inc(rescaled, 1)

            def step(i, k, known):
                if has(known, 0):
                    x1_mean(i, k % RING)
                if has(known, 2):
                    x_scale(i + 2, (k + 2) % RING)
                if has(known, -1):
                    gains(i - 1, (k - 1) % RING)
                if has(known, 3):
                    if has(known, 1):
                        alone(pool, y_turned, 2 * i + 4)
                    negate(i + 3, (k + 3) % RING)
                    if known == -3:
                        x_mean(0, 0)
                        pool.wait_ge(gates_set, 2)
                    gated_max(i + 3, (k + 3) % RING)
                if has(known, -1):
                    rescale(i - 1, (k - 1) % RING)
                if has(known, 0):
                    x1_scale(i, k % RING)
                if has(known, 3) and known != -3:
                    x_mean(i + 3, (k + 3) % RING)

            steps(pool, step)

        @block.scalar
        def _(act):
            def gates():
                act.wait_ge(small_loaded, 48)
                nc.scalar.activation(gx[:, :], gx_raw[:, :], ACT.Tanh).then_inc(gates_set, 1)
                nc.scalar.activation(gf[:, :], gf_raw[:, :], ACT.Tanh).then_inc(gates_set, 1)

            def query(t, s):
                act.wait_ge(nb1_set, t + 1)
                nc.scalar.activation(q[:, s % 2, :], x_in[:, s, :], ACT.Exp, bias=nb1[:, s:s + 1],
                                     scale=r1[:, s:s + 1]).then_inc(q_set, 1)

            def expert_exp(t, s):
                act.wait_ge(nmax_set, t + 1)
                nc.scalar.activation(e[:, s % 2, :], lg[:, s % 2, :], ACT.Exp, bias=nmax[:, s:s + 1],
                                     accum_out=tot[:, s:s + 1]).then_inc(e_set, 1)

            def take_x1(t, s):
                for h in range(2):
                    act.wait_ge(x1_turned, 2 * t + h + 1)
                    nc.scalar.copy(x1T[:, s % 2, HC * h:HC * h + HC, :],
                                   turn[h][:, :].rearrange("p (c n) -> p c n", c=HC)).then_inc(x1T_set, 1)

            def take_parts(t, s):
                act.wait_ge(parts_done, t + 1)
                nc.scalar.copy(parts[:, :], parts_p).then_inc(parts_set, 1)

            def take_w(t, s):
                act.wait_ge(w_turned, t + 1)
                nc.scalar.copy(wT[:, s % 2, :], wT_p).then_inc(wT_set, 1)

            def take_y(t, s, h):
                src = turn[h][:, :].rearrange("p (c n) -> p c n", c=HC)
                act.wait_ge(y_turned, 2 * t + h + 1)
                nc.scalar.activation(pT[:, s % 2, HC * h:HC * h + HC, :], src, ACT.Exp, scale=-1.0).then_inc(y_taken, 1)
                nc.scalar.copy(yT[:, s % 2, HC * h:HC * h + HC, :, 0:CT],
                               turn[h][:, :].rearrange("p (c t n) -> p c t n", c=HC, t=TILES)).then_inc(y_taken, 1)

            def x_sum(t, s):
                act.wait_ge(x_loaded[s], load_count(t, s))
                nc.scalar.activation(x_copy[:, :], x_in[:, s, :], ACT.Copy,
                                     accum_out=xsum[:, s:s + 1]).then_inc(x_summed, 1)

            def x_square(t, s):
                act.wait_ge(nm1_set, t + 1)
                nc.scalar.activation(x_squares[:, :], x_in[:, s, :], ACT.Square, bias=nm1[:, s:s + 1], scale=1.0 / ROOT,
                                     accum_out=var1[:, s:s + 1]).then_inc(x_squared, 1)

            def square(t, s):
                act.wait_ge(nm2_set, t + 1)
                nc.scalar.activation(squares[:, :], x1[:, s, :], ACT.Square, bias=nm2[:, s:s + 1], scale=1.0 / ROOT,
                                     accum_out=var2[:, s:s + 1]).then_inc(squared, 1)

            def step(i, k, known):
                if has(known, -1):
                    take_parts(i - 1, (k - 1) % RING)
                if has(known, 1):
                    if has(known, -1):
                        act.wait_ge(attended, 3 * i)
                    query(i + 1, (k + 1) % RING)
                if has(known, 2):
                    if has(known, 0):
                        act.wait_ge(kv_done, i + 1)
                    take_y(i + 2, (k + 2) % RING, 0)
                if has(known, -1):
                    expert_exp(i - 1, (k - 1) % RING)
                if has(known, 2):
                    take_y(i + 2, (k + 2) % RING, 1)
                    x_square(i + 2, (k + 2) % RING)
                if has(known, 0):
                    take_x1(i, k % RING)
                if has(known, -1):
                    take_w(i - 1, (k - 1) % RING)
                if has(known, 0):
                    square(i, k % RING)
                if has(known, 3):
                    x_sum(i + 3, (k + 3) % RING)
                if known == -3:
                    gates()

            steps(act, step)

        @block.vector
        def _(dve):
            def gate_mask():
                dve.wait_ge(consts_set, 1)
                dve.wait_ge(gates_set, 2)
                nc.vector.tensor_scalar(maskg[:, :], mask[:, :, :].rearrange("p h d -> p (h d)"), gx[:, 0:1], -1.0,
                                        ALU.mult, ALU.mult).then_inc(tables_set, 1)

            def router_centre():
                dve.wait_ge(w_loaded, 32)
                for h in range(2):
                    nc.vector.bn_stats(rw_stats[:, h, :], rw[:, HALF * h:HALF * h + HALF]).then_inc(rw_step, 1)
                dve.wait_ge(rw_step, 2)
                nc.vector.bn_aggr(rw_mv[:, :], rw_stats[:, :, :]).then_inc(rw_step, 1)
                dve.wait_ge(rw_step, 3)
                nc.vector.tensor_scalar(rwc[:, :], rw[:, :], rw_mv[:, 0:1], None, ALU.subtract).then_inc(rw_step, 1)
                nc.vector.tensor_scalar(eb[:, :], eb_raw[:, :], gf[0:E, 0:1], None, ALU.mult).then_inc(tables_set, 1)

            def router_take():
                dve.wait_ge(rw_turned, 1)
                nc.vector.tensor_copy(rwT[:, :, :], mixp[1][:, 0:CH * E].rearrange("p (c e) -> p c e", c=CH)
                                      ).then_inc(tables_set, 1)

            def sums(g):
                a, b = GROUPS[g]
                return attp[g % 2][:, 0:(b - a) * AW].rearrange("p (c w) -> p c w", c=b - a)

            def invert(t, s, g):
                a, b = GROUPS[g]
                dve.wait_ge(attended, 3 * t + g + 1)
                nc.vector.reciprocal(rG[:, s % 2, a:b, :], sums(g)[:, :, C:AW]).then_inc(rG_set, 1)

            def divide(t, s, g):
                a, b = GROUPS[g]
                dve.wait_ge(rG_set, 3 * t + g + 1)
                nc.vector.tensor_tensor(att[:, s % 2, a:b, :].rearrange("p c (h d) -> p c h d", h=HEADS),
                                        sums(g)[:, :, 0:C].rearrange("p c (h d) -> p c h d", h=HEADS),
                                        rG[:, s % 2, a:b, :].unsqueeze(3).broadcast_to([P, b - a, HEADS, DH]),
                                        ALU.mult).then_inc(divided, 1)

            def add(t, s, h):
                cols = slice(HALF * h, HALF * h + HALF)
                if h == 0:
                    dve.wait_ge(stored[s], load_count(t, s))
                    dve.wait_ge(gm_set, t + 1)
                dve.wait_ge(turned_back, 2 * t + h + 1)
                nc.vector.scalar_tensor_tensor(out=x1[:, s, cols], in0=x_in[:, s, cols], scalar=gm[:, s:s + 1],
                                               in1=back[h][:, :], op0=ALU.add, op1=ALU.add,
                                               accum_out=rowsum[:, s, h:h + 1]).then_inc(added, 1)

            def final(t, s, h):
                cols = slice(HALF * h, HALF * h + HALF)
                if h == 0:
                    dve.wait_ge(rescaled, t + 1)
                dve.wait_ge(mixed, 2 * t + h + 1)
                nc.vector.tensor_tensor(x1[:, s, cols], mixp[h][:, :], x1[:, s, cols], ALU.add).then_inc(finished, 1)

            def ctx_max(t, s):
                dve.wait_ge(c_loaded[s], load_count(t, s))
                nc.vector.tensor_reduce(m[:, s:s + 1], c_in[:, s, :], AX_X, ALU.max).then_inc(maxed, 1)

            def invert_kv(t, s):
                dve.wait_ge(kv_done, t + 1)
                nc.vector.reciprocal(rS[:, s % 2:s % 2 + 1], kvp[:, CT:KVN]).then_inc(rS_set, 1)

            def weights(t, s):
                dve.wait_ge(rS_set, t + 1)
                nc.vector.scalar_tensor_tensor(out=W[:, s % 2, 0:C].rearrange("p (t n) -> p t n", t=TILES),
                                               in0=kvp[:, 0:CT].unsqueeze(1).broadcast_to([P, TILES, CT]),
                                               scalar=rS[:, s % 2:s % 2 + 1],
                                               in1=maskg[:, :].rearrange("p (t n) -> p t n", t=TILES),
                                               op0=ALU.mult, op1=ALU.mult).then_inc(W_set, 1)

            def logits(t, s):
                dve.wait_ge(logits_done, t + 1)
                dve.wait_ge(r2_set, t + 1)
                nc.vector.scalar_tensor_tensor(out=lg[:, s % 2, :], in0=logit_p, scalar=r2[:, s:s + 1],
                                               in1=rb[:, :], op0=ALU.mult, op1=ALU.add).then_inc(lg_set, 1)

            def logit_max(t, s):
                dve.wait_ge(lg_set, t + 1)
                nc.vector.tensor_reduce(nmax[:, s:s + 1], lg[:, s % 2, :], AX_X, ALU.max,
                                        negate=True).then_inc(nmax_set, 1)

            def invert_total(t, s):
                dve.wait_ge(e_set, t + 1)
                nc.vector.reciprocal(rtot[:, s:s + 1], tot[:, s:s + 1]).then_inc(rtot_set, 1)

            def scores(t, s):
                dve.wait_ge(rtot_set, t + 1)
                nc.vector.tensor_scalar(score[:, s % 2, :], e[:, s % 2, :], rtot[:, s:s + 1], None,
                                        ALU.mult).then_inc(score_set, 1)

            def find_top(t, s):
                alone(dve, score_set, t + 1)
                nc.vector.max(top8[:, s % 2, :], score[:, s % 2, :]).then_inc(top8_set, 1)

            def drop_top(t, s):
                alone(dve, top8_set, t + 1)
                nc.vector.match_replace(rest[:, s % 2, :], top8[:, s % 2, :], score[:, s % 2, :], 0.0).then_inc(rest_set, 1)

            def keep_top(t, s):
                dve.wait_ge(rest_set, t + 1)
                nc.vector.scalar_tensor_tensor(out=wx[:, s % 2, :], in0=score[:, s % 2, :], scalar=1.0,
                                               in1=rest[:, s % 2, :], op0=ALU.mult, op1=ALU.subtract,
                                               accum_out=wsum[:, s:s + 1]).then_inc(kept, 1)

            def step(i, k, known):
                b, f, c, n = k % RING, (k - 1) % RING, (k - 2) % RING, (k + 1) % RING
                if has(known, 0):
                    invert(i, b, 0)
                    invert(i, b, 1)
                    divide(i, b, 0)
                    divide(i, b, 1)
                if has(known, -2):
                    final(i - 2, c, 0)
                if has(known, 0):
                    invert(i, b, 2)
                if has(known, 0):
                    divide(i, b, 2)
                if has(known, -1):
                    logits(i - 1, f)
                if has(known, -1):
                    logit_max(i - 1, f)
                if has(known, 0):
                    add(i, b, 0)
                if has(known, -1):
                    invert_total(i - 1, f)
                if has(known, 0):
                    add(i, b, 1)
                if has(known, -1):
                    scores(i - 1, f)
                if known == -3:
                    ctx_max(0, 0)
                    gate_mask()
                if has(known, 1):
                    invert_kv(i + 1, n)
                if has(known, -1):
                    find_top(i - 1, f)
                if has(known, 1):
                    weights(i + 1, n)
                if has(known, -1):
                    drop_top(i - 1, f)
                if has(known, -1):
                    keep_top(i - 1, f)
                if has(known, 3) and known != -3:
                    ctx_max(i + 3, (k + 3) % RING)
                if has(known, -2):
                    final(i - 2, c, 1)
                if known == -2:
                    router_centre()
                if known == -1:
                    router_take()

            steps(dve, step)

        @block.tensor
        def _(pe):
            pe.wait_ge(ident_set, 1)

            def turn_y(t, s):
                pe.wait_ge(negated, t + 1)
                for h in range(2):
                    for j in range(HC):
                        col = HALF * h + P * j
                        last = nc.tensor.transpose(turn[h][:, P * j:P * j + P], y[:, s % 2, col:col + P], ident[:, :])
                    last.then_inc(y_turned, 1)

            def kvs(t, s):
                pe.wait_ge(y_taken, 4 * t + 4)
                for ch in range(CH):
                    for g in range(TILES):
                        rows = slice(CT * g, CT * g + CT)
                        last = nc.tensor.matmul(kvp[rows, :], pT[:, s % 2, ch, rows], yT[:, s % 2, ch, g, :],
                                                start=(ch == 0), stop=(ch == CH - 1))
                last.then_inc(kv_done, 1)

            def attend(t, s, g):
                a, b = GROUPS[g]
                for ch in range(a, b):
                    o = (ch - a) * AW
                    last = nc.tensor.matmul(attp[g % 2][:, o:o + AW], q[:, s % 2, P * ch:P * ch + P],
                                            W[:, s % 2, :], start=True, stop=True)
                last.then_inc(attended, 1)

            def first_attend(t, s):
                pe.wait_ge(q_set, t + 1)
                pe.wait_ge(W_set, t + 1)
                attend(t, s, 0)

            def centred_turn():
                pe.wait_ge(rw_step, 4)
                for ch in range(CH):
                    last = nc.tensor.transpose(mixp[1][:, E * ch:E * ch + E], rwc[:, P * ch:P * ch + P],
                                               ident[0:E, 0:E])
                last.then_inc(rw_turned, 1)

            def turn_back(t, s, h, known):
                if h == 0 and has(known, -2):
                    pe.wait_ge(finished, 2 * (t - 2) + 1)
                elif has(known, -1):
                    pe.wait_ge(added, 2 * (t - 1) + h + 1)
                pe.wait_ge(divided, 3 * t + 2 + h)
                for j in range(HC):
                    last = nc.tensor.transpose(back[h][:, P * j:P * j + P], att[:, s % 2, HC * h + j, :], ident[:, :])
                last.then_inc(turned_back, 1)

            def turn_x1(t, s):
                for h in range(2):
                    pe.wait_ge(added, 2 * t + h + 1)
                    for j in range(HC):
                        col = HALF * h + P * j
                        last = nc.tensor.transpose(turn[h][:, P * j:P * j + P], x1[:, s, col:col + P], ident[:, :])
                    last.then_inc(x1_turned, 1)

            def route(t, s):
                for ch in range(CH):
                    if ch % HC == 0:
                        pe.wait_ge(x1T_set, 2 * t + ch // HC + 1)
                    odd = ch % 2
                    last = nc.tensor.matmul(parts_p[E * odd:E * odd + E, :], rwT[:, ch, :], x1T[:, s % 2, ch, :],
                                            start=(ch < 2), stop=(ch >= CH - 2))
                last.then_inc(parts_done, 1)

            def fold_parts(t, s):
                pe.wait_ge(parts_set, t + 1)
                nc.tensor.matmul(logit_p, parts[:, :], fold[:, :], start=True, stop=True).then_inc(logits_done, 1)

            def turn_w(t, s):
                alone(pe, kept, t + 1)
                nc.tensor.transpose(wT_p, wx[:, s % 2, :], ident[:, :]).then_inc(w_turned, 1)

            def mix(t, s, h):
                pe.wait_ge(wT_set, t + 1)
                nc.tensor.matmul(mixp[h][:, :], wT[:, s % 2, :], eb[:, HALF * h:HALF * h + HALF],
                                 start=True, stop=True).then_inc(mixed, 1)

            def step(i, k, known):
                b, c, n = k % RING, (k - 2) % RING, (k + 1) % RING
                if known == -1:
                    kvs(0, 0)
                    first_attend(0, 0)
                    attend(0, 0, 1)
                    centred_turn()
                if has(known, 0):
                    pe.wait_ge(divided, 3 * i + 1)
                    attend(i, b, 2)
                if has(known, -1):
                    fold_parts(i - 1, (k - 1) % RING)
                if has(known, 2):
                    if has(known, -1):
                        pe.wait_ge(x1T_set, 2 * i)
                    elif has(known, 1):
                        pe.wait_ge(y_taken, 4 * i + 8)
                    turn_y(i + 2, (k + 2) % RING)
                if has(known, 0):
                    turn_back(i, b, 0, known)
                    turn_back(i, b, 1, known)
                if has(known, 1) and known != -1:
                    pe.wait_ge(W_set, i + 1)
                    if has(known, -1):
                        pe.wait_ge(lg_set, i)
                    kvs(i + 1, n)
                if has(known, -2):
                    if has(known, -3):
                        pe.wait_ge(finished, 2 * i - 4)
                    mix(i - 2, c, 1)
                if has(known, 0):
                    if has(known, 2):
                        pe.wait_ge(y_taken, 4 * i + 12)
                    turn_x1(i, b)
                if has(known, -1):
                    if not has(known, 1):
                        pe.wait_ge(lg_set, i)
                    turn_w(i - 1, (k - 1) % RING)
                if has(known, 1) and known != -1:
                    pe.wait_ge(divided, 3 * i + 3)
                    first_attend(i + 1, n)
                    attend(i + 1, n, 1)
                if has(known, -1):
                    if has(known, 0):
                        pe.wait_ge(added, 2 * i + 1)
                    else:
                        pe.wait_ge(finished, 2 * i - 3)
                    mix(i - 1, (k - 1) % RING, 0)
                if has(known, 0):
                    if known == 0:
                        pe.wait_ge(tables_set, 3)
                    if has(known, -1):
                        pe.wait_ge(wT_set, i)
                    route(i, b)

            steps(pe, step)


_INS = ['x', 'ctx_4096', 'g_xattn', 'g_ffn', 'L0_ffn_router_weight', 'L0_ffn_router_bias', 'L0_ffn_expert_bias']
_OUT = ((16, 128, 1024), 'float32')


def kernel(**inputs):
    import numpy as _np
    import concourse.bacc as _bacc
    from concourse import mybir as _mybir
    from concourse.bass_utils import run_bass_kernel_spmd as _run

    nc = _bacc.Bacc("TRN2", target_bir_lowering=False, num_devices=1)
    arrays, args = {}, []
    for name in _INS:
        a = _np.ascontiguousarray(inputs[name])
        arrays[f"in_{name}_dram"] = a
        args.append(nc.dram_tensor(f"in_{name}_dram", a.shape, _mybir.dt.from_np(a.dtype), kind="ExternalInput").ap())
    shape, dtype = _OUT
    args.append(nc.dram_tensor("out_dram", shape, _mybir.dt.from_np(_np.dtype(dtype)), kind="ExternalOutput").ap())
    flamingo_block(nc, *args)
    r = _run(nc, [arrays], core_ids=[0])
    return r.results[0]["out_dram"]
```

```python
from contextlib import ExitStack

import concourse.bass as bass
from concourse import mybir

F32 = mybir.dt.float32
BF16 = mybir.dt.bfloat16
ALU = mybir.AluOpType
ACT = mybir.ActivationFunctionType
AX_X = mybir.AxisListType.X

P = 128
HEADS = 8
TOP = 8
EPS = 1e-5
HALF = 512
UNROLL = 4
RING = 4


def flamingo_block(nc, x, ctx_in, g_xattn, g_ffn, router_w, router_b, expert_b, out):
    B, C, N = x.shape
    E = router_w.shape[0]
    DH = C // HEADS
    CH = N // P
    HC = HALF // P
    CT = 32
    TILES = C // CT
    KVN = CT + 1
    AW = C + HEADS
    GROUPS = [(0, 3), (3, 6), (6, 8)]
    ROOT = float(N) ** 0.5
    FIRST, LOOPS = 2, (B - 5) // UNROLL
    LAST = FIRST + LOOPS * UNROLL
    X, Y, Z = B - 3, B - 2, B - 1
    assert C == P and 2 * E == P and N == 2 * HALF and CH == 8 and B % RING == 0

    with ExitStack() as stack:
        def sb(name, shape, dtype=F32):
            return stack.enter_context(nc.sbuf_tensor(name, shape, dtype))

        def bank(name):
            return stack.enter_context(nc.psum_tensor(name, [P, HALF], F32))

        def sem(name):
            return stack.enter_context(nc.semaphore(name))

        x_in = sb("x_in", [P, RING, N])
        c_in = sb("c_in", [P, RING, N])
        x1 = sb("x1", [P, RING, N])
        y = sb("y", [P, 2, N])
        pT = sb("pT", [P, 2, CH, C])
        yT = sb("yT", [P, 2, CH, TILES, KVN])
        q = sb("q", [P, 2, N])
        W = sb("W", [P, 2, AW])
        att = sb("att", [P, 2, CH, C])
        x1T = sb("x1T", [P, 2, CH, C])
        wx_parts = sb("wx_parts", [P, 2, 4, E], BF16)
        wT = sb("wT", [2 * E, 2, 2, C], BF16)
        x_copy = sb("x_copy", [P, 2, N])
        x_squares = sb("x_squares", [P, 2, N])
        squares = sb("squares", [P, 2, N])
        xsum = sb("xsum", [P, RING])
        nm1 = sb("nm1", [P, RING])
        var1 = sb("var1", [P, RING])
        ve1 = sb("ve1", [P, RING])
        r1 = sb("r1", [P, RING])
        nb1 = sb("nb1", [P, RING])
        m = sb("m", [P, RING])
        gm = sb("gm", [P, RING])
        rS = sb("rS", [P, 2])
        rG = sb("rG", [P, 2, CH, HEADS])
        rowsum = sb("rowsum", [P, RING, 2])
        nm2 = sb("nm2", [P, RING])
        var2 = sb("var2", [P, RING])
        ve2 = sb("ve2", [P, RING])
        r2 = sb("r2", [P, RING])
        parts = sb("parts", [2 * E, C])
        lg = sb("lg", [P, 2, E])
        nmax = sb("nmax", [P, RING])
        e = sb("e", [P, 2, E])
        tot = sb("tot", [P, RING])
        rtot = sb("rtot", [P, RING])
        score = sb("score", [P, 2, E])
        top8 = sb("top8", [P, 2, TOP])
        rest = sb("rest", [P, 2, E])
        wx = sb("wx", [P, 2, E])
        wx_rest = sb("wx_rest", [P, E])
        wsum = sb("wsum", [P, RING])
        gain = sb("gain", [P, RING])
        A = sb("A", [P, RING])
        shift = sb("shift", [P, RING])
        ident = sb("ident", [P, P])
        fold = sb("fold", [2 * E, E])
        mask = sb("mask", [P, HEADS, DH])
        maskg = sb("maskg", [P, C])
        half_neg = sb("half_neg", [P, 1])
        gx_raw = sb("gx_raw", [P, 1])
        gf_raw = sb("gf_raw", [P, 1])
        gx = sb("gx", [P, 1])
        gf = sb("gf", [P, 1])
        rb = sb("rb", [P, E])
        rw = sb("rw", [E, N])
        rwc = sb("rwc", [E, N])
        rwT = sb("rwT", [P, CH, E])
        rw_stats = sb("rw_stats", [E, 2, 6])
        rw_mv = sb("rw_mv", [E, 2])
        eb_raw = sb("eb_raw", [2 * E, N])
        eb = sb("eb", [2 * E, N])
        eb_rest = sb("eb_rest", [2 * E, N])
        eb_high = sb("eb_high", [2 * E, N], BF16)
        eb_mid = sb("eb_mid", [2 * E, N], BF16)
        eb_high_low = sb("eb_high_low", [2 * E, N], BF16)
        ident16 = sb("ident16", [P, P], BF16)

        turn = [bank("turn0"), bank("turn1")]
        attp = [bank("attp0"), bank("attp1")]
        back = [bank("back0"), bank("back1")]
        mixp = [back[0], bank("mix1")]
        small = bank("small")
        kvp = small[:, 0:KVN]
        parts_p = small[:, E:E + C]
        logit_p = small[:, E + C:2 * E + C]
        wT_p = mixp[1][:, 0:2 * C]
        wT_last = [attp[1][:, 0:2 * C], attp[0][:, 0:2 * C]]
        mix_last = [turn[0], turn[1]]

        x_loaded = [sem(f"x_loaded{s}") for s in range(RING)]
        c_loaded = [sem(f"c_loaded{s}") for s in range(RING)]
        stored = [sem(f"stored{s}") for s in range(RING)]
        small_loaded = sem("small_loaded")
        w_loaded = sem("w_loaded")
        zeros_set = sem("zeros_set")
        ident_set = sem("ident_set")
        consts_set = sem("consts_set")
        gates_set = sem("gates_set")
        rw_step = sem("rw_step")
        rw_turned = sem("rw_turned")
        tables_set = sem("tables_set")
        eb_step = sem("eb_step")
        maxed = sem("maxed")
        negated = sem("negated")
        gm_set = sem("gm_set")
        y_turned = sem("y_turned")
        y_taken = sem("y_taken")
        kv_done = sem("kv_done")
        rS_set = sem("rS_set")
        W_set = sem("W_set")
        x_summed = sem("x_summed")
        nm1_set = sem("nm1_set")
        x_squared = sem("x_squared")
        ve1_set = sem("ve1_set")
        r1_set = sem("r1_set")
        nb1_set = sem("nb1_set")
        q_set = sem("q_set")
        attended = sem("attended")
        rG_set = sem("rG_set")
        divided = sem("divided")
        turned_back = sem("turned_back")
        added = sem("added")
        nm2_set = sem("nm2_set")
        squared = sem("squared")
        ve2_set = sem("ve2_set")
        r2_set = sem("r2_set")
        x1_turned = sem("x1_turned")
        x1T_set = sem("x1T_set")
        parts_done = sem("parts_done")
        parts_set = sem("parts_set")
        logits_done = sem("logits_done")
        lg_set = sem("lg_set")
        nmax_set = sem("nmax_set")
        e_set = sem("e_set")
        rtot_set = sem("rtot_set")
        score_set = sem("score_set")
        top8_set = sem("top8_set")
        rest_set = sem("rest_set")
        kept = sem("kept")
        wx_split = sem("wx_split")
        gain_set = sem("gain_set")
        shift_set = sem("shift_set")
        rescaled = sem("rescaled")
        w_turned = sem("w_turned")
        wT_set = sem("wT_set")
        mixed = sem("mixed")
        finished = sem("finished")

        block = stack.enter_context(nc.Block())

        def steps(eng, start, step, finish):
            start()
            for i in range(1, FIRST):
                step(i, i, i)
            with eng.Fori(0, LOOPS) as j:
                for k in range(FIRST, FIRST + UNROLL):
                    step(j * UNROLL + k, k, None)
            for i in range(LAST, B - 1):
                step(i, i, i)
            finish()

        def alone(eng, semaphore, value):
            count = value if isinstance(value, int) else eng.to_reg(value)
            eng.wait_ge(consts_set, 1)
            eng.wait_ge(semaphore, count)

        def load_count(t, s):
            return (t - s) * (16 // RING) + 16

        def has(known, off):
            return known is None or 0 <= known + off < B

        @block.sync
        def _(sp):
            def load(ring, src, t, s, done):
                sp.dma_start(ring[:, s, :], src[t]).then_inc(done[s], 16)

            load(c_in, ctx_in, 0, 0, c_loaded)
            load(x_in, x, 0, 0, x_loaded)
            sp.dma_start(gx_raw[:, :], g_xattn.rearrange("(a b) -> a b", a=1).broadcast_to([P, 1])).then_inc(small_loaded, 16)
            sp.dma_start(gf_raw[:, :], g_ffn.rearrange("(a b) -> a b", a=1).broadcast_to([P, 1])).then_inc(small_loaded, 16)
            sp.dma_start(rb[:, :], router_b.rearrange("(a b) -> a b", a=1).broadcast_to([P, E])).then_inc(small_loaded, 16)
            load(c_in, ctx_in, 1, 1, c_loaded)
            sp.dma_start(rw[:, :], router_w).then_inc(w_loaded, 16)
            for k in range(2):
                sp.dma_start(eb_raw[E * k:E * k + E, :], expert_b).then_inc(w_loaded, 16)
            load(x_in, x, 1, 1, x_loaded)
            for t in (2, 3):
                load(c_in, ctx_in, t, t, c_loaded)
                load(x_in, x, t, t, x_loaded)
            for s in range(RING):
                sp.sem_inc(stored[s], 16)

            def load_c(t, s):
                sp.wait_ge(negated, t - RING + 1)
                load(c_in, ctx_in, t, s, c_loaded)

            def load_x(t, s):
                sp.wait_ge(added, 2 * (t - RING) + 2)
                load(x_in, x, t, s, x_loaded)

            def store(t, s):
                sp.wait_ge(finished, 2 * t + 2)
                sp.dma_start(out[t], x1[:, s, :]).then_inc(stored[s], 16)

            SP_LOOPS = (B - 7 - FIRST) // UNROLL
            for i in range(-3, FIRST):
                if i >= 0:
                    load_x(i + 4, i % RING)
                load_c(i + 7, (i + 7) % RING)
            with sp.Fori(0, SP_LOOPS) as j:
                for k in range(FIRST, FIRST + UNROLL):
                    i = j * UNROLL + k
                    load_x(i + 4, k % RING)
                    store(i - 2, (k - 2) % RING)
                    load_c(i + 7, (k + 7) % RING)
            for i in range(FIRST + SP_LOOPS * UNROLL, B + 1):
                if i + 4 < B:
                    load_x(i + 4, i % RING)
                store(i - 2, (i - 2) % RING)
                if i + 7 < B:
                    load_c(i + 7, (i + 7) % RING)
            for h in range(2):
                cols = slice(HALF * h, HALF * h + HALF)
                sp.wait_ge(finished, 2 * Z + h + 1)
                sp.dma_start(out[Z][:, cols], x1[:, Z % RING, cols]).then_inc(stored[Z % RING], 16)
            for s in range(RING):
                sp.wait_ge(stored[s], 16 * (1 + B // RING + (s == Z % RING)))

        @block.gpsimd
        def _(pool):
            nc.gpsimd.memset(ident[:, :], 0.0).then_inc(zeros_set, 1)
            nc.gpsimd.memset(mask[:, :, :], 1.0).then_inc(zeros_set, 1)
            nc.gpsimd.memset(W[:, :, C:AW], 1.0).then_inc(zeros_set, 1)
            nc.gpsimd.memset(half_neg[:, :], -0.5).then_inc(zeros_set, 1)
            nc.gpsimd.memset(yT[:, :, :, :, CT:KVN], 1.0).then_inc(zeros_set, 1)
            nc.gpsimd.memset(fold[:, :], 0.0).then_inc(zeros_set, 1)
            pool.wait_ge(zeros_set, 6)
            nc.gpsimd.affine_select(out=ident[:, :], in_=ident[:, :], compare_op=ALU.not_equal, fill=1.0,
                                    base=0, pattern=[[-1, P]], channel_multiplier=1).then_inc(ident_set, 1)
            nc.gpsimd.affine_select(out=mask[:, :, :], in_=mask[:, :, :], compare_op=ALU.is_ge, fill=0.0,
                                    base=0, pattern=[[-DH, HEADS], [0, DH]], channel_multiplier=1).then_inc(zeros_set, 1)
            nc.gpsimd.affine_select(out=W[:, :, C:AW], in_=W[:, :, C:AW], compare_op=ALU.is_ge, fill=0.0,
                                    base=0, pattern=[[0, 2], [-DH, HEADS]], channel_multiplier=1).then_inc(zeros_set, 1)
            nc.gpsimd.affine_select(out=fold[:, :], in_=fold[:, :], compare_op=ALU.not_equal, fill=1.0,
                                    base=0, pattern=[[-1, E]], channel_multiplier=1).then_inc(zeros_set, 1)
            pool.wait_ge(zeros_set, 9)
            nc.gpsimd.affine_select(out=mask[:, :, :], in_=mask[:, :, :], compare_op=ALU.is_ge, fill=0.0,
                                    base=DH - 1, pattern=[[DH, HEADS], [0, DH]], channel_multiplier=-1).then_inc(zeros_set, 1)
            nc.gpsimd.affine_select(out=W[:, :, C:AW], in_=W[:, :, C:AW], compare_op=ALU.is_ge, fill=0.0,
                                    base=DH - 1, pattern=[[0, 2], [DH, HEADS]], channel_multiplier=-1).then_inc(zeros_set, 1)
            nc.gpsimd.affine_select(out=fold[:, :], in_=fold[:, :], compare_op=ALU.not_equal, fill=1.0,
                                    base=-E, pattern=[[-1, E]], channel_multiplier=1).then_inc(zeros_set, 1)
            pool.wait_ge(ident_set, 1)
            nc.gpsimd.tensor_scalar(ident16[:, :], ident[:, :], 1.0, 0.0, ALU.mult, ALU.add).then_inc(zeros_set, 1)
            pool.wait_ge(zeros_set, 13)
            nc.gpsimd.tensor_copy(mask[0:1, 0:1, 0:1], mask[0:1, 0:1, 0:1]).then_inc(consts_set, 1)

            def negate(t, s):
                alone(pool, maxed, t + 1)
                nc.gpsimd.tensor_scalar(y[:, s % 2, :], c_in[:, s, :], -1.0, m[:, s:s + 1],
                                        ALU.mult, ALU.add).then_inc(negated, 1)

            def gated_max(t, s):
                nc.gpsimd.tensor_scalar(gm[:, s:s + 1], m[:, s:s + 1], gx[:, 0:1], 1.0,
                                        ALU.mult, ALU.mult).then_inc(gm_set, 1)

            def x_mean(t, s):
                alone(pool, x_summed, t + 1)
                nc.gpsimd.tensor_scalar(nm1[:, s:s + 1], xsum[:, s:s + 1], -1.0 / (N * ROOT), 0.0,
                                        ALU.mult, ALU.add).then_inc(nm1_set, 1)

            def x_scale(t, s):
                alone(pool, x_squared, t + 1)
                nc.gpsimd.tensor_scalar(ve1[:, s:s + 1], var1[:, s:s + 1], EPS, 1.0,
                                        ALU.add, ALU.mult).then_inc(ve1_set, 1)
                alone(pool, ve1_set, t + 1)
                nc.gpsimd.tensor_tensor(r1[:, s:s + 1], ve1[:, s:s + 1], half_neg[:, :], ALU.pow).then_inc(r1_set, 1)
                alone(pool, r1_set, t + 1)
                nc.gpsimd.tensor_scalar(nb1[:, s:s + 1], nm1[:, s:s + 1], r1[:, s:s + 1], ROOT,
                                        ALU.mult, ALU.mult).then_inc(nb1_set, 1)

            def x1_scale(t, s):
                alone(pool, squared, t + 1)
                nc.gpsimd.tensor_scalar(ve2[:, s:s + 1], var2[:, s:s + 1], EPS, 1.0,
                                        ALU.add, ALU.mult).then_inc(ve2_set, 1)
                alone(pool, ve2_set, t + 1)
                nc.gpsimd.tensor_tensor(r2[:, s:s + 1], ve2[:, s:s + 1], half_neg[:, :], ALU.pow).then_inc(r2_set, 1)

            def rescale(t, s, cols=slice(0, N)):
                alone(pool, shift_set, 2 * t + 2)
                pool.wait_ge(squared, t + 1)
                pool.wait_ge(x1_turned, 2 * t + 2)
                nc.gpsimd.tensor_scalar(x1[:, s, cols], x1[:, s, cols], A[:, s:s + 1], shift[:, s:s + 1],
                                        ALU.mult, ALU.add).then_inc(rescaled, 1)

            def split_high():
                pool.wait_ge(eb_step, 1)
                nc.gpsimd.tensor_scalar(eb_high[:, :], eb[:, :], 1.0, 0.0, ALU.mult, ALU.add).then_inc(eb_step, 1)

            def split_rest():
                pool.wait_ge(eb_step, 2)
                nc.gpsimd.tensor_tensor(eb_rest[:, :], eb[:, :], eb_high[:, :], ALU.subtract).then_inc(eb_step, 1)

            def split_mid():
                pool.wait_ge(eb_step, 3)
                nc.gpsimd.tensor_scalar(eb_mid[:, :], eb_rest[:, :], 1.0, 0.0, ALU.mult, ALU.add).then_inc(eb_step, 1)

            def split_low():
                pool.wait_ge(eb_step, 4)
                nc.gpsimd.tensor_tensor(eb_high_low[:, :], eb_rest[:, :], eb_mid[:, :], ALU.subtract).then_inc(eb_step, 1)
                pool.wait_ge(eb_step, 5)
                nc.gpsimd.tensor_scalar(eb_high_low[0:E, :], eb_high[0:E, :], 1.0, 0.0, ALU.mult, ALU.add).then_inc(eb_step, 1)
                pool.wait_ge(eb_step, 6)

            def split_kept_high(t, s):
                alone(pool, kept, t + 1)
                nc.gpsimd.tensor_scalar(wx_parts[:, s % 2, 0:4:3, :],
                                        wx[:, s % 2, :].unsqueeze(1).broadcast_to([P, 2, E]), 1.0, 0.0,
                                        ALU.mult, ALU.add).then_inc(wx_split, 1)

            def split_kept_rest(t, s):
                alone(pool, wx_split, 4 * t + 1)
                nc.gpsimd.tensor_tensor(wx_rest[:, :], wx[:, s % 2, :], wx_parts[:, s % 2, 0, :],
                                        ALU.subtract).then_inc(wx_split, 1)

            def split_kept_mid(t, s):
                alone(pool, wx_split, 4 * t + 2)
                nc.gpsimd.tensor_scalar(wx_parts[:, s % 2, 1, :], wx_rest[:, :], 1.0, 0.0,
                                        ALU.mult, ALU.add).then_inc(wx_split, 1)

            def split_kept_low(t, s):
                alone(pool, wx_split, 4 * t + 3)
                nc.gpsimd.tensor_tensor(wx_parts[:, s % 2, 2, :], wx_rest[:, :], wx_parts[:, s % 2, 1, :],
                                        ALU.subtract).then_inc(wx_split, 1)

            def start():
                negate(0, 0)
                x_mean(0, 0)
                x_scale(0, 0)
                pool.wait_ge(gates_set, 2)
                gated_max(0, 0)
                negate(1, 1)
                gated_max(1, 1)
                x_mean(1, 1)
                alone(pool, y_turned, 2)
                negate(2, 2)
                gated_max(2, 2)
                x_scale(1, 1)
                x_mean(2, 2)
                split_high()
                split_rest()
                alone(pool, y_turned, 4)
                negate(3, 3)
                gated_max(3, 3)
                x_scale(2, 2)
                x1_scale(0, 0)
                x_mean(3, 3)
                split_mid()
                split_low()

            def step(i, k, known):
                s, f = k % RING, (k - 1) % RING
                split_kept_high(i - 1, f)
                split_kept_rest(i - 1, f)
                split_kept_mid(i - 1, f)
                split_kept_low(i - 1, f)
                rescale(i - 1, f)
                if has(known, 3):
                    alone(pool, y_turned, 2 * i + 4)
                    negate(i + 3, (k + 3) % RING)
                x1_scale(i, s)
                if has(known, 3):
                    gated_max(i + 3, (k + 3) % RING)
                    x_mean(i + 3, (k + 3) % RING)
                if has(known, 2):
                    x_scale(i + 2, (k + 2) % RING)

            def finish():
                x1_scale(Z, Z % RING)
                rescale(Y, Y % RING)
                rescale(Z, Z % RING, slice(HALF, N))

            steps(pool, start, step, finish)

        @block.scalar
        def _(act):
            def gates():
                act.wait_ge(small_loaded, 48)
                nc.scalar.activation(gx[:, :], gx_raw[:, :], ACT.Tanh).then_inc(gates_set, 1)
                nc.scalar.activation(gf[:, :], gf_raw[:, :], ACT.Tanh).then_inc(gates_set, 1)

            def query(t, s):
                act.wait_ge(nb1_set, t + 1)
                nc.scalar.activation(q[:, s % 2, :], x_in[:, s, :], ACT.Exp, bias=nb1[:, s:s + 1],
                                     scale=r1[:, s:s + 1]).then_inc(q_set, 1)

            def expert_exp(t, s):
                act.wait_ge(nmax_set, t + 1)
                nc.scalar.activation(e[:, s % 2, :], lg[:, s % 2, :], ACT.Exp, bias=nmax[:, s:s + 1],
                                     accum_out=tot[:, s:s + 1]).then_inc(e_set, 1)

            def take_x1(t, s, h):
                act.wait_ge(x1_turned, 2 * t + h + 1)
                nc.scalar.copy(x1T[:, s % 2, HC * h:HC * h + HC, :],
                               turn[h][:, :].rearrange("p (c n) -> p c n", c=HC)).then_inc(x1T_set, 1)

            def take_parts(t, s):
                act.wait_ge(parts_done, t + 1)
                nc.scalar.copy(parts[:, :], parts_p).then_inc(parts_set, 1)

            def take_w(t, s, src):
                act.wait_ge(w_turned, t + 1)
                nc.scalar.copy(wT[:, s % 2, :, :], src.rearrange("p (k c) -> p k c", k=2)).then_inc(wT_set, 1)

            def take_y(t, s, h):
                src = turn[h][:, :].rearrange("p (c n) -> p c n", c=HC)
                act.wait_ge(y_turned, 2 * t + h + 1)
                nc.scalar.activation(pT[:, s % 2, HC * h:HC * h + HC, :], src, ACT.Exp, scale=-1.0).then_inc(y_taken, 1)
                nc.scalar.copy(yT[:, s % 2, HC * h:HC * h + HC, :, 0:CT],
                               turn[h][:, :].rearrange("p (c t n) -> p c t n", c=HC, t=TILES)).then_inc(y_taken, 1)

            def x_sum(t, s):
                act.wait_ge(x_loaded[s], load_count(t, s))
                nc.scalar.activation(x_copy[:, s % 2, :], x_in[:, s, :], ACT.Copy,
                                     accum_out=xsum[:, s:s + 1]).then_inc(x_summed, 1)

            def x_square(t, s):
                act.wait_ge(nm1_set, t + 1)
                nc.scalar.activation(x_squares[:, s % 2, :], x_in[:, s, :], ACT.Square, bias=nm1[:, s:s + 1], scale=1.0 / ROOT,
                                     accum_out=var1[:, s:s + 1]).then_inc(x_squared, 1)

            def square(t, s):
                act.wait_ge(nm2_set, t + 1)
                nc.scalar.activation(squares[:, s % 2, :], x1[:, s, :], ACT.Square, bias=nm2[:, s:s + 1], scale=1.0 / ROOT,
                                     accum_out=var2[:, s:s + 1]).then_inc(squared, 1)

            def rescale_half(t, s):
                act.wait_ge(shift_set, 2 * t + 2)
                nc.scalar.activation(x1[:, s, 0:HALF], x1[:, s, 0:HALF], ACT.Identity, bias=shift[:, s:s + 1],
                                     scale=A[:, s:s + 1]).then_inc(rescaled, 1)

            def start():
                x_sum(0, 0)
                gates()
                x_square(0, 0)
                take_y(0, 0, 0)
                take_y(0, 0, 1)
                query(0, 0)
                x_sum(1, 1)
                take_y(1, 1, 0)
                take_y(1, 1, 1)
                x_square(1, 1)
                x_sum(2, 2)
                query(1, 1)
                act.wait_ge(kv_done, 1)
                take_y(2, 2, 0)
                take_y(2, 2, 1)
                x_square(2, 2)
                take_x1(0, 0, 0)
                take_x1(0, 0, 1)
                square(0, 0)
                x_sum(3, 3)

            def step(i, k, known):
                s, f = k % RING, (k - 1) % RING
                take_parts(i - 1, f)
                if has(known, 3):
                    x_sum(i + 3, (k + 3) % RING)
                if has(known, 2):
                    act.wait_ge(kv_done, i + 1)
                    take_y(i + 2, (k + 2) % RING, 0)
                expert_exp(i - 1, f)
                if has(known, 2):
                    take_y(i + 2, (k + 2) % RING, 1)
                act.wait_ge(attended, 3 * i)
                query(i + 1, (k + 1) % RING)
                take_x1(i, s, 0)
                take_x1(i, s, 1)
                square(i, s)
                if has(known, 2):
                    x_square(i + 2, (k + 2) % RING)

            def finish():
                take_parts(Y, Y % RING)
                expert_exp(Y, Y % RING)
                take_x1(Z, Z % RING, 0)
                take_x1(Z, Z % RING, 1)
                square(Z, Z % RING)
                take_parts(Z, Z % RING)
                take_w(Y, Y % RING, wT_last[0])
                expert_exp(Z, Z % RING)
                rescale_half(Z, Z % RING)
                take_w(Z, Z % RING, wT_last[1])

            steps(act, start, step, finish)

        @block.vector
        def _(dve):
            def gate_mask():
                dve.wait_ge(consts_set, 1)
                dve.wait_ge(gates_set, 2)
                nc.vector.tensor_scalar(maskg[:, :], mask[:, :, :].rearrange("p h d -> p (h d)"), gx[:, 0:1], -1.0,
                                        ALU.mult, ALU.mult).then_inc(tables_set, 1)

            def router_centre():
                dve.wait_ge(w_loaded, 48)
                for h in range(2):
                    nc.vector.bn_stats(rw_stats[:, h, :], rw[:, HALF * h:HALF * h + HALF]).then_inc(rw_step, 1)
                dve.wait_ge(rw_step, 2)
                nc.vector.bn_aggr(rw_mv[:, :], rw_stats[:, :, :]).then_inc(rw_step, 1)
                dve.wait_ge(rw_step, 3)
                nc.vector.tensor_scalar(rwc[:, :], rw[:, :], rw_mv[:, 0:1], None, ALU.subtract).then_inc(rw_step, 1)

            def gate_biases():
                nc.vector.tensor_scalar(eb[:, :], eb_raw[:, :], gf[:, 0:1], None, ALU.mult).then_inc(eb_step, 1)

            def router_take():
                dve.wait_ge(rw_turned, 1)
                nc.vector.tensor_copy(rwT[:, :, :], mixp[1][:, 0:CH * E].rearrange("p (c e) -> p c e", c=CH)
                                      ).then_inc(tables_set, 1)

            def sums(g):
                a, b = GROUPS[g]
                return attp[g % 2][:, 0:(b - a) * AW].rearrange("p (c w) -> p c w", c=b - a)

            def invert(t, s, g):
                a, b = GROUPS[g]
                dve.wait_ge(attended, 3 * t + g + 1)
                nc.vector.reciprocal(rG[:, s % 2, a:b, :], sums(g)[:, :, C:AW]).then_inc(rG_set, 1)

            def divide(t, s, g):
                a, b = GROUPS[g]
                dve.wait_ge(rG_set, 3 * t + g + 1)
                nc.vector.tensor_tensor(att[:, s % 2, a:b, :].rearrange("p c (h d) -> p c h d", h=HEADS),
                                        sums(g)[:, :, 0:C].rearrange("p c (h d) -> p c h d", h=HEADS),
                                        rG[:, s % 2, a:b, :].unsqueeze(3).broadcast_to([P, b - a, HEADS, DH]),
                                        ALU.mult).then_inc(divided, 1)

            def add(t, s, h):
                cols = slice(HALF * h, HALF * h + HALF)
                if h == 0:
                    dve.wait_ge(stored[s], load_count(t, s))
                    dve.wait_ge(gm_set, t + 1)
                dve.wait_ge(turned_back, 2 * t + h + 1)
                nc.vector.scalar_tensor_tensor(out=x1[:, s, cols], in0=x_in[:, s, cols], scalar=gm[:, s:s + 1],
                                               in1=back[h][:, :], op0=ALU.add, op1=ALU.add,
                                               accum_out=rowsum[:, s, h:h + 1]).then_inc(added, 1)

            def x1_mean(t, s):
                dve.wait_ge(added, 2 * t + 2)
                nc.vector.tensor_scalar(nm2[:, s:s + 1], rowsum[:, s, 0:1], rowsum[:, s, 1:2], -1.0 / (N * ROOT),
                                        ALU.add, ALU.mult).then_inc(nm2_set, 1)

            def gain_of(t, s):
                dve.wait_ge(kept, t + 1)
                nc.vector.scalar_tensor_tensor(out=gain[:, s:s + 1], in0=wsum[:, s:s + 1], scalar=gf[:, 0:1],
                                               in1=r2[:, s:s + 1], op0=ALU.mult, op1=ALU.mult).then_inc(gain_set, 1)

            def scale_and_shift(t, s):
                dve.wait_ge(gain_set, t + 1)
                nc.vector.tensor_scalar(shift[:, s:s + 1], nm2[:, s:s + 1], gain[:, s:s + 1], ROOT,
                                        ALU.mult, ALU.mult).then_inc(shift_set, 1)
                nc.vector.tensor_scalar(A[:, s:s + 1], gain[:, s:s + 1], 1.0, None, ALU.add).then_inc(shift_set, 1)

            def final(t, s, h, parts=1, mixp=mixp):
                cols = slice(HALF * h, HALF * h + HALF)
                if h == 0:
                    dve.wait_ge(rescaled, t + parts)
                dve.wait_ge(mixed, 2 * t + h + 1)
                nc.vector.tensor_tensor(x1[:, s, cols], mixp[h][:, :], x1[:, s, cols], ALU.add).then_inc(finished, 1)

            def ctx_max(t, s):
                dve.wait_ge(c_loaded[s], load_count(t, s))
                nc.vector.tensor_reduce(m[:, s:s + 1], c_in[:, s, :], AX_X, ALU.max).then_inc(maxed, 1)

            def invert_kv(t, s):
                dve.wait_ge(kv_done, t + 1)
                nc.vector.reciprocal(rS[:, s % 2:s % 2 + 1], kvp[:, CT:KVN]).then_inc(rS_set, 1)

            def weights(t, s):
                dve.wait_ge(rS_set, t + 1)
                nc.vector.scalar_tensor_tensor(out=W[:, s % 2, 0:C].rearrange("p (t n) -> p t n", t=TILES),
                                               in0=kvp[:, 0:CT].unsqueeze(1).broadcast_to([P, TILES, CT]),
                                               scalar=rS[:, s % 2:s % 2 + 1],
                                               in1=maskg[:, :].rearrange("p (t n) -> p t n", t=TILES),
                                               op0=ALU.mult, op1=ALU.mult).then_inc(W_set, 1)

            def logits(t, s):
                dve.wait_ge(logits_done, t + 1)
                dve.wait_ge(r2_set, t + 1)
                nc.vector.scalar_tensor_tensor(out=lg[:, s % 2, :], in0=logit_p, scalar=r2[:, s:s + 1],
                                               in1=rb[:, :], op0=ALU.mult, op1=ALU.add).then_inc(lg_set, 1)

            def logit_max(t, s):
                dve.wait_ge(lg_set, t + 1)
                nc.vector.tensor_reduce(nmax[:, s:s + 1], lg[:, s % 2, :], AX_X, ALU.max,
                                        negate=True).then_inc(nmax_set, 1)

            def invert_total(t, s):
                dve.wait_ge(e_set, t + 1)
                nc.vector.reciprocal(rtot[:, s:s + 1], tot[:, s:s + 1]).then_inc(rtot_set, 1)

            def scores(t, s):
                dve.wait_ge(rtot_set, t + 1)
                nc.vector.tensor_scalar(score[:, s % 2, :], e[:, s % 2, :], rtot[:, s:s + 1], None,
                                        ALU.mult).then_inc(score_set, 1)

            def find_top(t, s):
                alone(dve, score_set, t + 1)
                nc.vector.max(top8[:, s % 2, :], score[:, s % 2, :]).then_inc(top8_set, 1)

            def drop_top(t, s):
                alone(dve, top8_set, t + 1)
                nc.vector.match_replace(rest[:, s % 2, :], top8[:, s % 2, :], score[:, s % 2, :], 0.0).then_inc(rest_set, 1)

            def keep_top(t, s):
                dve.wait_ge(rest_set, t + 1)
                nc.vector.scalar_tensor_tensor(out=wx[:, s % 2, :], in0=score[:, s % 2, :], scalar=1.0,
                                               in1=rest[:, s % 2, :], op0=ALU.mult, op1=ALU.subtract,
                                               accum_out=wsum[:, s:s + 1]).then_inc(kept, 1)

            def take_w(t, s):
                dve.wait_ge(w_turned, t + 1)
                nc.vector.tensor_copy(wT[:, s % 2, :, :], wT_p.rearrange("p (k c) -> p k c", k=2)).then_inc(wT_set, 1)

            def split_and_gain(t, s):
                dve.wait_ge(kept, t + 1)
                nc.vector.tensor_copy(wx_parts[:, s % 2, 0:4:3, :],
                                      wx[:, s % 2, :].unsqueeze(1).broadcast_to([P, 2, E])).then_inc(wx_split, 1)
                gain_of(t, s)
                dve.wait_ge(wx_split, 4 * t + 1)
                nc.vector.tensor_tensor(wx_rest[:, :], wx[:, s % 2, :], wx_parts[:, s % 2, 0, :],
                                        ALU.subtract).then_inc(wx_split, 1)
                scale_and_shift(t, s)
                dve.wait_ge(wx_split, 4 * t + 2)
                nc.vector.tensor_copy(wx_parts[:, s % 2, 1, :], wx_rest[:, :]).then_inc(wx_split, 1)
                dve.wait_ge(wx_split, 4 * t + 3)
                nc.vector.tensor_tensor(wx_parts[:, s % 2, 2, :], wx_rest[:, :], wx_parts[:, s % 2, 1, :],
                                        ALU.subtract).then_inc(wx_split, 1)

            def start():
                ctx_max(0, 0)
                gate_mask()
                ctx_max(1, 1)
                router_centre()
                invert_kv(0, 0)
                weights(0, 0)
                ctx_max(2, 2)
                gate_biases()
                invert(0, 0, 0)
                invert(0, 0, 1)
                divide(0, 0, 0)
                divide(0, 0, 1)
                router_take()
                invert(0, 0, 2)
                invert_kv(1, 1)
                divide(0, 0, 2)
                weights(1, 1)
                add(0, 0, 0)
                add(0, 0, 1)
                x1_mean(0, 0)
                ctx_max(3, 3)
                invert(1, 1, 0)
                divide(1, 1, 0)
                invert(1, 1, 1)
                divide(1, 1, 1)

            def step(i, k, known):
                b, f, c, n = k % RING, (k - 1) % RING, (k - 2) % RING, (k + 1) % RING
                invert(i, b, 2)
                if has(known, -2):
                    final(i - 2, c, 0)
                divide(i, b, 2)
                logits(i - 1, f)
                logit_max(i - 1, f)
                add(i, b, 0)
                invert_total(i - 1, f)
                add(i, b, 1)
                scores(i - 1, f)
                invert_kv(i + 1, n)
                x1_mean(i, b)
                find_top(i - 1, f)
                weights(i + 1, n)
                drop_top(i - 1, f)
                keep_top(i - 1, f)
                if has(known, 3):
                    ctx_max(i + 3, (k + 3) % RING)
                gain_of(i - 1, f)
                invert(i + 1, n, 0)
                scale_and_shift(i - 1, f)
                if has(known, -2):
                    final(i - 2, c, 1)
                divide(i + 1, n, 0)
                invert(i + 1, n, 1)
                take_w(i - 1, f)
                divide(i + 1, n, 1)

            def finish():
                x_, y_, z = X % RING, Y % RING, Z % RING
                invert(Z, z, 2)
                final(X, x_, 0)
                divide(Z, z, 2)
                logits(Y, y_)
                logit_max(Y, y_)
                add(Z, z, 0)
                invert_total(Y, y_)
                add(Z, z, 1)
                scores(Y, y_)
                x1_mean(Z, z)
                find_top(Y, y_)
                drop_top(Y, y_)
                keep_top(Y, y_)
                final(X, x_, 1)
                split_and_gain(Y, y_)
                logits(Z, z)
                logit_max(Z, z)
                final(Y, y_, 0)
                invert_total(Z, z)
                scores(Z, z)
                find_top(Z, z)
                drop_top(Z, z)
                keep_top(Z, z)
                split_and_gain(Z, z)
                final(Y, y_, 1)
                final(Z, z, 0, 2, mix_last)
                final(Z, z, 1, 2, mix_last)

            steps(dve, start, step, finish)

        @block.tensor
        def _(pe):
            pe.wait_ge(ident_set, 1)

            def turn_y(t, s):
                pe.wait_ge(negated, t + 1)
                for h in range(2):
                    for j in range(HC):
                        col = HALF * h + P * j
                        last = nc.tensor.transpose(turn[h][:, P * j:P * j + P], y[:, s % 2, col:col + P], ident[:, :])
                    last.then_inc(y_turned, 1)

            def kvs(t, s):
                for ch in range(CH):
                    if ch % HC == 0:
                        pe.wait_ge(y_taken, 4 * t + 2 * (ch // HC) + 2)
                    for g in range(TILES):
                        rows = slice(CT * g, CT * g + CT)
                        last = nc.tensor.matmul(kvp[rows, :], pT[:, s % 2, ch, rows], yT[:, s % 2, ch, g, :],
                                                start=(ch == 0), stop=(ch == CH - 1))
                last.then_inc(kv_done, 1)

            def attend(t, s, g):
                a, b = GROUPS[g]
                for ch in range(a, b):
                    o = (ch - a) * AW
                    last = nc.tensor.matmul(attp[g % 2][:, o:o + AW], q[:, s % 2, P * ch:P * ch + P],
                                            W[:, s % 2, :], start=True, stop=True)
                last.then_inc(attended, 1)

            def first_attend(t, s):
                pe.wait_ge(q_set, t + 1)
                pe.wait_ge(W_set, t + 1)
                attend(t, s, 0)

            def centred_turn():
                pe.wait_ge(rw_step, 4)
                for ch in range(CH):
                    last = nc.tensor.transpose(mixp[1][:, E * ch:E * ch + E], rwc[:, P * ch:P * ch + P],
                                               ident[0:E, 0:E])
                last.then_inc(rw_turned, 1)

            def turn_back(t, s, h):
                pe.wait_ge(divided, 3 * t + 2 + h)
                for j in range(HC):
                    last = nc.tensor.transpose(back[h][:, P * j:P * j + P], att[:, s % 2, HC * h + j, :], ident[:, :])
                last.then_inc(turned_back, 1)

            def turn_x1(t, s, h):
                pe.wait_ge(added, 2 * t + h + 1)
                for j in range(HC):
                    col = HALF * h + P * j
                    last = nc.tensor.transpose(turn[h][:, P * j:P * j + P], x1[:, s, col:col + P], ident[:, :])
                last.then_inc(x1_turned, 1)

            def route(t, s):
                for ch in range(CH):
                    if ch % HC == 0:
                        pe.wait_ge(x1T_set, 2 * t + ch // HC + 1)
                    odd = ch % 2
                    last = nc.tensor.matmul(parts_p[E * odd:E * odd + E, :], rwT[:, ch, :], x1T[:, s % 2, ch, :],
                                            start=(ch < 2), stop=(ch >= CH - 2))
                last.then_inc(parts_done, 1)

            def fold_parts(t, s):
                pe.wait_ge(parts_set, t + 1)
                nc.tensor.matmul(logit_p, parts[:, :], fold[:, :], start=True, stop=True).then_inc(logits_done, 1)

            def turn_w(t, s, dst=wT_p):
                pe.wait_ge(wx_split, 4 * t + 4)
                for k in range(2):
                    last = nc.tensor.matmul(dst[:, C * k:C * k + C],
                                            wx_parts[:, s % 2, 2 * k:2 * k + 2, :].rearrange("p k e -> p (k e)"),
                                            ident16[:, :], start=True, stop=True)
                last.then_inc(w_turned, 1)

            def mix(t, s, h, mixp=mixp):
                cols = slice(HALF * h, HALF * h + HALF)
                if h == 0:
                    pe.wait_ge(wT_set, t + 1)
                nc.tensor.matmul(mixp[h][:, :], wT[:, s % 2, 0, :], eb_high[:, cols], start=True, stop=False)
                nc.tensor.matmul(mixp[h][:, :], wT[:, s % 2, 0, :], eb_mid[:, cols], start=False, stop=False)
                nc.tensor.matmul(mixp[h][:, :], wT[:, s % 2, 1, :], eb_high_low[:, cols],
                                 start=False, stop=True).then_inc(mixed, 1)

            def start():
                turn_y(0, 0)
                kvs(0, 0)
                turn_y(1, 1)
                first_attend(0, 0)
                attend(0, 0, 1)
                centred_turn()
                pe.wait_ge(y_taken, 8)
                turn_y(2, 2)
                pe.wait_ge(divided, 1)
                attend(0, 0, 2)
                kvs(1, 1)
                turn_back(0, 0, 0)
                turn_back(0, 0, 1)
                pe.wait_ge(y_taken, 12)
                turn_x1(0, 0, 0)
                turn_x1(0, 0, 1)
                first_attend(1, 1)
                attend(1, 1, 1)
                pe.wait_ge(tables_set, 2)
                route(0, 0)

            def step(i, k, known):
                b, f, c, n = k % RING, (k - 1) % RING, (k - 2) % RING, (k + 1) % RING
                pe.wait_ge(divided, 3 * i + 1)
                attend(i, b, 2)
                if has(known, -2):
                    if known is None and k == FIRST:
                        pe.wait_ge(eb_step, 6)
                    pe.wait_ge(added, 2 * i - 1)
                    mix(i - 2, c, 0)
                fold_parts(i - 1, f)
                if has(known, 2):
                    pe.wait_ge(x1T_set, 2 * i)
                    turn_y(i + 2, (k + 2) % RING)
                if has(known, -2):
                    pe.wait_ge(finished, 2 * i - 3)
                turn_back(i, b, 0)
                pe.wait_ge(added, 2 * i)
                turn_back(i, b, 1)
                pe.wait_ge(lg_set, i)
                kvs(i + 1, n)
                if has(known, -2):
                    mix(i - 2, c, 1)
                if has(known, 2):
                    pe.wait_ge(y_taken, 4 * i + 12)
                turn_x1(i, b, 0)
                turn_x1(i, b, 1)
                pe.wait_ge(divided, 3 * i + 3)
                first_attend(i + 1, n)
                attend(i + 1, n, 1)
                route(i, b)
                if has(known, -2):
                    pe.wait_ge(finished, 2 * i - 2)
                turn_w(i - 1, f)

            def finish():
                x_, y_, z = X % RING, Y % RING, Z % RING
                pe.wait_ge(divided, 3 * Z + 1)
                attend(Z, z, 2)
                fold_parts(Y, y_)
                pe.wait_ge(added, 2 * Y + 1)
                mix(X, x_, 0)
                pe.wait_ge(finished, 2 * X + 1)
                turn_back(Z, z, 0)
                turn_back(Z, z, 1)
                mix(X, x_, 1)
                pe.wait_ge(x1T_set, 2 * Z)
                turn_x1(Z, z, 0)
                turn_x1(Z, z, 1)
                pe.wait_ge(lg_set, Y + 1)
                route(Z, z)
                fold_parts(Z, z)
                pe.wait_ge(divided, 3 * Z + 3)
                turn_w(Y, y_, wT_last[0])
                mix(Y, y_, 0)
                pe.wait_ge(finished, 2 * X + 2)
                mix(Y, y_, 1)
                turn_w(Z, z, wT_last[1])
                pe.wait_ge(x1T_set, 2 * Z + 2)
                mix(Z, z, 0, mix_last)
                mix(Z, z, 1, mix_last)

            steps(pe, start, step, finish)


_INS = ['x', 'ctx_4096', 'g_xattn', 'g_ffn', 'L0_ffn_router_weight', 'L0_ffn_router_bias', 'L0_ffn_expert_bias']
_OUT = ((16, 128, 1024), 'float32')


def kernel(**inputs):
    import numpy as _np
    import concourse.bacc as _bacc
    from concourse import mybir as _mybir
    from concourse.bass_utils import run_bass_kernel_spmd as _run

    nc = _bacc.Bacc("TRN2", target_bir_lowering=False, num_devices=1)
    arrays, args = {}, []
    for name in _INS:
        a = _np.ascontiguousarray(inputs[name])
        arrays[f"in_{name}_dram"] = a
        args.append(nc.dram_tensor(f"in_{name}_dram", a.shape, _mybir.dt.from_np(a.dtype), kind="ExternalInput").ap())
    shape, dtype = _OUT
    args.append(nc.dram_tensor("out_dram", shape, _mybir.dt.from_np(_np.dtype(dtype)), kind="ExternalOutput").ap())
    flamingo_block(nc, *args)
    r = _run(nc, [arrays], core_ids=[0])
    return r.results[0]["out_dram"]
```
